# Optimizing a Trainium2 kernel written in Bass

```python
import numpy as np
import jax
import jax.numpy as jnp

def _softmax(x, axis=-1):
    return jax.nn.softmax(x, axis=axis)

def _gelu(x):
    return jax.nn.gelu(x, approximate=True)

def _silu(x):
    return jax.nn.silu(x)

def _sigmoid(x):
    return jax.nn.sigmoid(x)

def _layernorm(x, axis=-1, eps=1e-05):
    m = jnp.mean(x, axis=axis, keepdims=True)
    v = jnp.var(x, axis=axis, keepdims=True)
    return (x - m) / jnp.sqrt(v + eps)

def _scatter_add(tgt, idx, src, axis=0):
    return tgt.at[idx].add(src)

def _segment_sum(src, seg, n):
    return jax.ops.segment_sum(src, seg, n)
kernel_name = 'mk_adj_resnorm_d4_adj_r2_bdc6b2'

def setup_inputs(seed: int=0):
    np.random.seed(seed)
    _w = jnp.asarray

    def _rec_inputs():
        import jax
        import jax.numpy as jnp
        _gk = jax.random.key(seed)
        x = -0.001547 + 1.001 * jax.random.normal(jax.random.fold_in(_gk, 1), (128, 128, 256), jnp.float32)
        _a = jax.random.bernoulli(jax.random.fold_in(_gk, 2), 0.125, (128, 128))
        _a = jnp.logical_or(_a, jnp.swapaxes(_a, -1, -2))
        _a = jnp.logical_or(_a, jnp.eye(128, dtype=bool))
        _af = _a.astype(jnp.float32)
        _af = _af * jax.random.uniform(jax.random.fold_in(_gk, 3), (128, 128), jnp.float32, 0.05, 0.237401)
        adj = _af
        return (x, adj)
    x, adj = _rec_inputs()

    def _L0_gnn_setup():
        import jax, jax.numpy as jnp
        import numpy as np
        key = jax.random.key(seed)
        k1, k2, k3, k4 = jax.random.split(key, 4)
        B, D, N = (4, 128, 256)
        scale = 1.0 / np.sqrt(2 * D)
        x = jax.random.normal(k1, (B, D, N), dtype=jnp.float32)
        W1 = jax.random.normal(k2, (D, D), dtype=jnp.float32) * scale
        W2 = jax.random.normal(k3, (D, D), dtype=jnp.float32) * scale
        b = jax.random.normal(k4, (D,), dtype=jnp.float32) * scale
        return {'x': x, 'W1': W1, 'W2': W2, 'b': b}
    _L0_gnn_all = _L0_gnn_setup()
    _L0_gnn_in = {k: v for k, v in _L0_gnn_all.items() if k in ('b',)}
    del _L0_gnn_all

    def _L1_gnn_setup():
        import jax, jax.numpy as jnp
        import numpy as np
        B, N, D, O = (8, 2048, 256, 256)
        key = jax.random.key(seed)
        k1, k2, k3, k4 = jax.random.split(key, 4)
        x = jax.random.normal(k1, (B, N, D), dtype=jnp.float32)
        adj = jax.random.uniform(k2, (N, N), dtype=jnp.float32)
        weight = jax.random.normal(k3, (D, O), dtype=jnp.float32) * 0.02
        bias = jax.random.normal(k4, (O,), dtype=jnp.float32) * 0.02
        return {'x': x, 'adj': adj, 'weight': weight, 'bias': bias}
    _L1_gnn_all = _L1_gnn_setup()
    _L1_gnn_in = {k: v for k, v in _L1_gnn_all.items() if k in ('weight', 'bias')}
    del _L1_gnn_all

    def _L2_gnn_setup():
        import jax, jax.numpy as jnp
        import numpy as np
        B, N, D, H = (16, 1025, 256, 8)
        LN_EPS = 1e-05

        def _make_mask(key, n):
            n_proto = n - 1
            adj = jax.random.bernoulli(key, 0.03, (n_proto, n_proto)).astype(jnp.float32)
            adj = jnp.clip(adj + adj.T + jnp.eye(n_proto, dtype=jnp.float32), 0.0, 1.0)
            mask = jnp.zeros((n, n), dtype=jnp.float32)
            mask = mask.at[0, :].set(1.0).at[:, 0].set(1.0)
            mask = mask.at[1:, 1:].set(adj)
            return mask
        key = jax.random.key(seed)
        ks = jax.random.split(key, 7)
        s = 1.0 / np.sqrt(D)
        return {'x': jax.random.normal(ks[0], (B, N, D), dtype=jnp.float32), 'w_qkv': jax.random.uniform(ks[1], (D, 3 * D), dtype=jnp.float32, minval=-s, maxval=s), 'w_proj': jax.random.uniform(ks[2], (D, D), dtype=jnp.float32, minval=-s, maxval=s), 'b_proj': jnp.zeros((D,), dtype=jnp.float32), 'ln_gamma': jnp.ones((D,), dtype=jnp.float32), 'ln_beta': jnp.zeros((D,), dtype=jnp.float32), 'attn_mask': _make_mask(ks[3], N)}
    _L2_gnn_all = _L2_gnn_setup()
    _L2_gnn_in = {k: v for k, v in _L2_gnn_all.items() if k in ('w_qkv', 'w_proj', 'b_proj', 'ln_gamma', 'ln_beta')}
    del _L2_gnn_all

    def _L3_gnn_setup():
        import jax, jax.numpy as jnp
        import numpy as np
        B, N, D, H = (4, 1024, 256, 8)
        HD = D // H
        key = jax.random.key(seed)
        ks = jax.random.split(key, 10)
        x = jax.random.normal(ks[0], (B, N, D), dtype=jnp.float32)
        adj = (jax.random.uniform(ks[1], (N, N)) < 0.1).astype(jnp.float32)
        s = 1.0 / np.sqrt(D)
        Wq = jax.random.normal(ks[2], (D, D), dtype=jnp.float32) * s
        Wk = jax.random.normal(ks[3], (D, D), dtype=jnp.float32) * s
        Wv = jax.random.normal(ks[4], (D, D), dtype=jnp.float32) * s
        Wo = jax.random.normal(ks[5], (D, D), dtype=jnp.float32) * s
        bq = jnp.zeros((D,), jnp.float32)
        bk = jnp.zeros((D,), jnp.float32)
        bv = jnp.zeros((D,), jnp.float32)
        bo = jnp.zeros((D,), jnp.float32)
        return {'x': x, 'adj': adj, 'Wq': Wq, 'bq': bq, 'Wk': Wk, 'bk': bk, 'Wv': Wv, 'bv': bv, 'Wo': Wo, 'bo': bo}
    _L3_gnn_all = _L3_gnn_setup()
    _L3_gnn_in = {k: v for k, v in _L3_gnn_all.items() if k in ('Wq', 'bq', 'Wk', 'bk', 'Wv', 'bv', 'Wo', 'bo')}
    del _L3_gnn_all
    return {'x': x, 'adj': adj, 'L0_gnn_b': _L0_gnn_in['b'], 'L1_gnn_weight': _L1_gnn_in['weight'], 'L1_gnn_bias': _L1_gnn_in['bias'], 'L2_gnn_w_qkv': _L2_gnn_in['w_qkv'], 'L2_gnn_w_proj': _L2_gnn_in['w_proj'], 'L2_gnn_b_proj': _L2_gnn_in['b_proj'], 'L2_gnn_ln_gamma': _L2_gnn_in['ln_gamma'], 'L2_gnn_ln_beta': _L2_gnn_in['ln_beta'], 'L3_gnn_Wq': _L3_gnn_in['Wq'], 'L3_gnn_bq': _L3_gnn_in['bq'], 'L3_gnn_Wk': _L3_gnn_in['Wk'], 'L3_gnn_bk': _L3_gnn_in['bk'], 'L3_gnn_Wv': _L3_gnn_in['Wv'], 'L3_gnn_bv': _L3_gnn_in['bv'], 'L3_gnn_Wo': _L3_gnn_in['Wo'], 'L3_gnn_bo': _L3_gnn_in['bo']}

def reference(x, adj, L0_gnn_b, L1_gnn_weight, L1_gnn_bias, L2_gnn_w_qkv, L2_gnn_w_proj, L2_gnn_b_proj, L2_gnn_ln_gamma, L2_gnn_ln_beta, L3_gnn_Wq, L3_gnn_bq, L3_gnn_Wk, L3_gnn_bk, L3_gnn_Wv, L3_gnn_bv, L3_gnn_Wo, L3_gnn_bo):
    import jax
    import jax.numpy as jnp

    def _L0_gnn_ref(x, W1, W2, b):
        import jax, jax.numpy as jnp
        import numpy as np
        A = jnp.einsum('od,bdn->bon', W1, x)
        C = jnp.einsum('od,bdn->bon', W2, x) + b[None, :, None]
        pre = A[:, :, None, :] + (C - A)[:, :, :, None]
        out = jnp.max(jax.nn.relu(pre), axis=-1)
        return out

    def _L1_gnn_ref(x, adj, weight, bias):
        import jax, jax.numpy as jnp
        import numpy as np
        B, N, D, O = (8, 2048, 256, 256)
        y = jnp.einsum('nm,bmd->bnd', adj, x)
        out = jnp.einsum('bnd,do->bno', y, weight) + bias
        return out

    def _L2_gnn_ref(x, w_qkv, w_proj, b_proj, ln_gamma, ln_beta, attn_mask):
        import jax, jax.numpy as jnp
        import numpy as np
        B, N, D, H = (16, 1025, 256, 8)
        LN_EPS = 1e-05

        def _make_mask(key, n):
            n_proto = n - 1
            adj = jax.random.bernoulli(key, 0.03, (n_proto, n_proto)).astype(jnp.float32)
            adj = jnp.clip(adj + adj.T + jnp.eye(n_proto, dtype=jnp.float32), 0.0, 1.0)
            mask = jnp.zeros((n, n), dtype=jnp.float32)
            mask = mask.at[0, :].set(1.0).at[:, 0].set(1.0)
            mask = mask.at[1:, 1:].set(adj)
            return mask
        b, n, d = x.shape
        hd = d // H
        scale = hd ** (-0.5)
        qkv = (x @ w_qkv).reshape(b, n, 3, H, hd).transpose(2, 0, 3, 1, 4)
        q, k, v = (qkv[0], qkv[1], qkv[2])
        attn = jnp.einsum('bhnd,bhmd->bhnm', q, k) * scale
        attn = jnp.where(attn_mask[None, None] == 0, -jnp.inf, attn)
        attn = jax.nn.softmax(attn, axis=-1)
        o = jnp.einsum('bhnm,bhmd->bhnd', attn, v).transpose(0, 2, 1, 3).reshape(b, n, d)
        o = o @ w_proj + b_proj
        mu = jnp.mean(o, axis=-1, keepdims=True)
        var = jnp.mean(jnp.square(o - mu), axis=-1, keepdims=True)
        ln = (o - mu) * jax.lax.rsqrt(var + LN_EPS) * ln_gamma + ln_beta
        return o + ln

    def _L3_gnn_ref(x, adj, Wq, bq, Wk, bk, Wv, bv, Wo, bo):
        import jax, jax.numpy as jnp
        import numpy as np
        B, N, D, H = (4, 1024, 256, 8)
        HD = D // H
        b, n, d = x.shape
        q = (x @ Wq + bq).reshape(b, n, H, HD)
        k = (x @ Wk + bk).reshape(b, n, H, HD)
        v = (x @ Wv + bv).reshape(b, n, H, HD)
        scores = jnp.einsum('bqhd,bkhd->bhqk', q, k) / jnp.sqrt(jnp.float32(HD))
        scores = scores + (1.0 - adj)[None, None, :, :] * -1000000000.0
        attn = jax.nn.softmax(scores, axis=-1)
        out = jnp.einsum('bhqk,bkhd->bqhd', attn, v).reshape(b, n, d)
        return out @ Wo + bo
    x = _layernorm(x + _L0_gnn_ref(x, adj, adj, L0_gnn_b), axis=-1)
    x = _layernorm(x + _L1_gnn_ref(x, adj, L1_gnn_weight, L1_gnn_bias), axis=-1)
    x = _layernorm(x + _L2_gnn_ref(x, L2_gnn_w_qkv, L2_gnn_w_proj, L2_gnn_b_proj, L2_gnn_ln_gamma, L2_gnn_ln_beta, adj), axis=-1)
    x = _layernorm(x + _L3_gnn_ref(x, adj, L3_gnn_Wq, L3_gnn_bq, L3_gnn_Wk, L3_gnn_bk, L3_gnn_Wv, L3_gnn_bv, L3_gnn_Wo, L3_gnn_bo), axis=-1)
    return x

_drawn_inputs = setup_inputs


def setup_inputs(seed=0):
    import zlib

    import numpy as np

    out = dict(_drawn_inputs(seed))
    spreads = {'L2_gnn_b_proj': (0.0, 0.1),
     'L2_gnn_ln_gamma': (1.0, 0.2),
     'L2_gnn_ln_beta': (0.0, 0.1),
     'L3_gnn_bq': (0.0, 0.1),
     'L3_gnn_bk': (0.0, 0.1),
     'L3_gnn_bv': (0.0, 0.1),
     'L3_gnn_bo': (0.0, 0.1)}
    factors = {}
    for name, (base, spread) in spreads.items():
        noise = np.random.default_rng([zlib.crc32(name.encode()), seed]).standard_normal(out[name].shape)
        drawn = base * np.exp(spread * noise) if base else spread * noise
        out[name] = jnp.asarray(drawn.astype(out[name].dtype))
    for name, factor in factors.items():
        out[name] = (out[name] * factor).astype(out[name].dtype)
    return out
```

```python
from contextlib import ExitStack

import concourse.bass as bass
from concourse import mybir

F32 = mybir.dt.float32
ALU = mybir.AluOpType
ACT = mybir.ActivationFunctionType
AX_X = mybir.AxisListType.X

P = 128
PAIR = 2
HEADS = 8
NEG_BIG = -1e30
LN_EPS = 1e-5

LAG = {"L0": 0, "L1": 1, "a": 2, "c": 3, "c_tail": 4}
LAST_LAG = 5

USES = [
    ("xT_a", "a"), ("q_a", "a"), ("k_a", "a"), ("v_a", "a"),
    ("pv_c", "c_tail"), ("proj_c", "c_tail"),
    ("yT", "L1"),
    ("xT_c", "c"), ("q_c", "c"), ("k_c", "c"), ("v_c", "c"),
    ("h1", "L1"), ("A0", "L0"),
    ("pv_a", "a"), ("proj_a", "a"),
]


def gnn_stack_kernel(nc, x, adj, b0, w1, b1, wqkv2, wp2, bp2, gam2, bet2,
                     wq3, bq3, wk3, bk3, wv3, bv3, wo3, bo3, out):
    B, N, D = x.shape
    HD = D // HEADS
    DC = D // P
    GROUPS = B // PAIR
    SCALE = float(HD) ** -0.5
    PERIOD = 2
    HEAD_TURNS = 3
    assert N == P and HD == 32 and DC == 2 and GROUPS % PERIOD == 0

    x_v = x.rearrange("(g b) m d -> g m b d", b=PAIR)
    out_v = out.rearrange("(g b) m d -> g m b d", b=PAIR)

    with ExitStack() as ctx:
        def sb(name, shape):
            return ctx.enter_context(nc.sbuf_tensor(name, shape, F32))

        def ps(name, shape):
            return ctx.enter_context(nc.psum_tensor(name, shape, F32))

        def sem(name):
            return ctx.enter_context(nc.semaphore(name))

        ident = sb("ident", [P, P])
        adj_sb = sb("adj_sb", [P, N])
        adjT = sb("adjT", [P, N])
        w1_sb = sb("w1_sb", [P, DC, D])
        wqkv2_sb = sb("wqkv2_sb", [P, DC, 3 * D])
        wq3_sb = sb("wq3_sb", [P, DC, D])
        wk3_sb = sb("wk3_sb", [P, DC, D])
        wv3_sb = sb("wv3_sb", [P, DC, D])
        wo_sb = {"a": sb("wp2_sb", [P, DC, D]), "c": sb("wo3_sb", [P, DC, D])}
        b0_col = sb("b0_col", [P, 1])
        bq_col = sb("bq_col", [P, DC])
        bk_col = sb("bk_col", [P, DC])
        bv_col = sb("bv_col", [P, DC])
        bv_wide = sb("bv_wide", [P, DC, P])
        b1_row = sb("b1_row", [P, D])
        bp2_row = sb("bp2_row", [P, D])
        gam_row = sb("gam_row", [P, D])
        bet_row = sb("bet_row", [P, D])
        bo_row = sb("bo_row", [P, D])
        neg_half = sb("neg_half", [P, PAIR])
        ones = sb("ones", [P, P])
        bias = {"a": sb("bias_a", [P, 2, N]), "c": sb("bias_c", [P, 2, N])}

        x0 = sb("x0", [P, 2, PAIR, D])
        t0 = sb("t0", [P, PAIR, D])
        mx0 = sb("mx0", [P, PAIR])
        r0 = sb("r0", [P, PAIR])
        x1 = sb("x1", [P, 2, PAIR, D])
        x1b = sb("x1b", [P, PAIR, D])
        yT = sb("yT_sb", [P, PAIR, DC, N])
        h1 = sb("h1_sb", [P, PAIR, D])
        x2 = sb("x2", [P, 2, PAIR, D])
        x2b = sb("x2b", [P, 2, PAIR, D])
        o_sb = sb("o_sb", [P, PAIR, D])
        ox = sb("ox", [P, PAIR, D])
        w_ln = sb("w_ln", [P, PAIR, D])
        h2 = sb("h2", [P, PAIR, D])
        x3 = sb("x3", [P, 2, PAIR, D])
        x3b = sb("x3b", [P, 2, PAIR, D])
        h3 = sb("h3", [P, PAIR, D])
        out_sb = sb("out_sb", [P, 2, PAIR, D])
        xin = {"a": x2, "c": x3}

        xT, qT, kT, v, t, E, nmax, esum, rinv = ({} for _ in range(9))
        for L in "ac":
            xT[L] = sb(f"xT_{L}_sb", [P, DC, PAIR * N])
            qT[L] = sb(f"qT_{L}_sb", [P, DC, PAIR * N])
            kT[L] = sb(f"kT_{L}_sb", [P, DC, PAIR * N])
            v[L] = sb(f"v_{L}_sb", [P, PAIR, D])
            t[L] = sb(f"t_{L}_sb", [P, PAIR, HEADS, N])
            E[L] = sb(f"E_{L}_sb", [P, PAIR, HEADS, N])
            nmax[L] = sb(f"nmax_{L}", [P, PAIR, HEADS])
            esum[L] = sb(f"esum_{L}", [P, PAIR, HEADS])
            rinv[L] = sb(f"rinv_{L}", [P, PAIR, HEADS])
        pT = [sb(f"pT_sb{c}", [P, 4, N]) for c in range(2)]
        oT = sb("oT", [P, PAIR, DC, N])

        gate = sb("gate", [P, 1])
        NORMS = ("n0", "n1", "ni", "no", "nc")
        st = {n: sb(f"st_{n}", [P, PAIR, 6]) for n in NORMS}
        mv = {n: sb(f"mv_{n}", [P, PAIR, 2]) for n in NORMS}
        ve = {n: sb(f"ve_{n}", [P, PAIR]) for n in NORMS}
        rstd = {n: sb(f"rstd_{n}", [P, PAIR]) for n in NORMS}

        S = ps("S", [P, 4, 512])
        PT = [ps(f"PT{c}", [P, 4, N]) for c in range(2)]
        GB = [ps(f"GB{k}", [P, 512]) for k in range(2)]

        s_w = sem("weights_loaded")
        s_ident = sem("ident_made")
        s_ones = sem("ones_made")
        s_setup = sem("setup_vector")
        s_adjT = sem("adjT_done")
        s_adjTc = sem("adjT_copied")
        s_bvwo = sem("bvwo_done")
        s_ready = sem("constants_ready")
        x_loaded = [sem(f"x_loaded{p}") for p in range(2)]
        stored = [sem(f"stored{p}") for p in range(2)]
        done = {u: sem(f"{u}_done") for u, _ in USES}
        drained = {u: sem(f"{u}_drained") for u, _ in USES}
        r0_made = sem("r0_made")
        mx0_made = sem("mx0_made")
        t0_made = sem("t0_made")
        x1_made = sem("x1_made")
        x1b_made = sem("x1b_made")
        x2_made = sem("x2_made")
        x2b_made = sem("x2b_made")
        ox_made = sem("ox_made")
        w_made = sem("w_made")
        h2_made = sem("h2_made")
        x3_made = sem("x3_made")
        x3b_made = sem("x3b_made")
        out_made = sem("out_made")
        xin_made = {"a": x2_made, "c": x3_made}
        s_done = {L: sem(f"scores_{L}_done") for L in "ac"}
        masked, maxed, exped, inverted, normed, pT_done, pT_copied = ({} for _ in range(7))
        for L in "ac":
            masked[L] = sem(f"masked_{L}")
            maxed[L] = sem(f"maxed_{L}")
            exped[L] = sem(f"exped_{L}")
            inverted[L] = sem(f"inverted_{L}")
            normed[L] = sem(f"normed_{L}")
            pT_done[L] = [sem(f"pT_{L}_done{c}") for c in range(2)]
            pT_copied[L] = [sem(f"pT_{L}_copied{c}") for c in range(2)]
        stats_made = {n: sem(f"stats_{n}") for n in NORMS}
        aggr_made = {n: sem(f"aggr_{n}") for n in NORMS}
        var_made = {n: sem(f"var_{n}") for n in NORMS}
        rstd_made = {n: sem(f"rstd_{n}") for n in NORMS}

        def runs(stage, rep):
            return 0 <= rep - LAG[stage] < GROUPS

        def engine_program(eng, body):
            for i in range(PERIOD * HEAD_TURNS):
                body(i, i)
            with eng.Fori(HEAD_TURNS, GROUPS // PERIOD) as turn:
                for p in range(PERIOD):
                    body(turn * PERIOD + p, PERIOD * HEAD_TURNS + p)
            for i in range(GROUPS, GROUPS + LAST_LAG):
                body(i, i)

        def bank(use, rep):
            at = [u for u, _ in USES].index(use)
            return GB[(rep * len(USES) + at) % 2]

        def wait_bank(pe, use, i, rep):
            n = rep * len(USES) + [u for u, _ in USES].index(use) - 2
            while n >= 0:
                before, stage = USES[n % len(USES)]
                then = n // len(USES)
                if runs(stage, then):
                    pe.wait_ge(drained[before], i - (rep - then) - LAG[stage] + 1)
                    return
                n -= 2

        block = ctx.enter_context(nc.Block())

        @block.sync
        def _(sp):
            sp.dma_start(adj_sb[:, :], adj).then_inc(s_w, 16)
            for dst, src in ((w1_sb, w1), (wqkv2_sb, wqkv2), (wo_sb["a"], wp2), (wq3_sb, wq3),
                             (wk3_sb, wk3), (wv3_sb, wv3), (wo_sb["c"], wo3)):
                sp.dma_start(dst[:, :, :], src.rearrange("(c p) n -> p c n", p=P)).then_inc(s_w, 16)
            sp.dma_start(b0_col[:, :], b0.rearrange("(p o) -> p o", o=1)).then_inc(s_w, 16)
            for dst, src in ((bq_col, bq3), (bk_col, bk3), (bv_col, bv3)):
                for c in range(DC):
                    sp.dma_start(dst[:, c:c + 1],
                                 src[c * P:(c + 1) * P].rearrange("(p o) -> p o", o=1)).then_inc(s_w, 16)
            for dst, src in ((b1_row, b1), (bp2_row, bp2), (gam_row, gam2), (bet_row, bet2), (bo_row, bo3)):
                sp.dma_start(dst[:, :], src.rearrange("(o n) -> o n", o=1).to_broadcast([P, D])).then_inc(s_w, 16)

            def body(i, rep):
                p = rep % 2
                if runs("L0", rep):
                    g = i
                    if rep >= 2:
                        sp.wait_ge(t0_made, 2 * (g - 1))
                    sp.dma_start(x0[:, p, :, :], x_v[g]).then_inc(x_loaded[p], 16)
                if 0 <= rep - LAST_LAG < GROUPS:
                    g = i - LAST_LAG
                    sp.wait_ge(out_made, 2 * (g + 1))
                    q = (rep - LAST_LAG) % 2
                    sp.dma_start(out_v[g], out_sb[:, q, :, :]).then_inc(stored[q], 16)

            engine_program(sp, body)
            for p in range(2):
                sp.wait_ge(stored[p], 16 * GROUPS // 2)

        N_WEIGHT_DMAS = 1 + 7 + 1 + 3 * DC + 5

        @block.tensor
        def _(pe):
            pe.wait_ge(s_ident, 2)
            pe.wait_ge(s_w, 16 * N_WEIGHT_DMAS)
            pe.transpose(GB[0][:, 0:P], adj_sb[:, :], ident[:, :]).then_inc(s_adjT, 1)
            pe.wait_ge(s_setup, 2)
            for c in range(DC):
                last = pe.matmul(GB[1][:, 0:D], bv_wide[:, c, :], wo_sb["c"][:, c, :],
                                 start=(c == 0), stop=(c == DC - 1))
            last.then_inc(s_bvwo, 1)
            pe.wait_ge(s_adjTc, 1)
            pe.wait_ge(s_ready, 1)

            def project_in(L, i, rep):
                if not runs(L, rep):
                    return
                g, p = i - LAG[L], (rep - LAG[L]) % 2
                if L == "a":
                    wq, wk, wv = (wqkv2_sb[:, :, n * D:(n + 1) * D] for n in range(3))
                else:
                    wq, wk, wv = wq3_sb[:, :, :], wk3_sb[:, :, :], wv3_sb[:, :, :]
                o = bank(f"xT_{L}", rep)
                wait_bank(pe, f"xT_{L}", i, rep)
                pe.wait_ge(xin_made[L], 2 * (g + 1))
                for c in range(DC):
                    for b in range(PAIR):
                        n = c * PAIR + b
                        last = pe.transpose(o[:, n * N:(n + 1) * N], xin[L][:, p, b, c * P:(c + 1) * P],
                                            ident[:, :])
                last.then_inc(done[f"xT_{L}"], 1)
                for use, w in ((f"q_{L}", wq), (f"k_{L}", wk)):
                    o = bank(use, rep)
                    wait_bank(pe, use, i, rep)
                    pe.wait_ge(drained[f"xT_{L}"], g + 1)
                    for m in range(DC):
                        for c in range(DC):
                            last = pe.matmul(o[:, m * PAIR * N:(m + 1) * PAIR * N], w[:, c, m * P:(m + 1) * P],
                                             xT[L][:, c, :], start=(c == 0), stop=(c == DC - 1))
                    last.then_inc(done[use], 1)
                o = bank(f"v_{L}", rep)
                wait_bank(pe, f"v_{L}", i, rep)
                for b in range(PAIR):
                    for c in range(DC):
                        last = pe.matmul(o[:, b * D:(b + 1) * D], xT[L][:, c, b * N:(b + 1) * N], wv[:, c, :],
                                         start=(c == 0), stop=(c == DC - 1))
                last.then_inc(done[f"v_{L}"], 1)

            def scores(L, i, rep):
                if not runs(L, rep):
                    return
                g = i - LAG[L]
                pe.wait_ge(drained[f"q_{L}"], g + 1)
                pe.wait_ge(drained[f"k_{L}"], g + 1)
                if L == "a" and runs("c", rep - 1):
                    pe.wait_ge(masked["c"], 2 * (i - 1 - LAG["c"] + 1))
                elif L == "a":
                    if rep - LAG["a"] >= 1:
                        pe.wait_ge(masked["a"], 2 * g)
                elif runs("a", rep):
                    pe.wait_ge(masked["a"], 2 * (i - LAG["a"] + 1))
                else:
                    pe.wait_ge(masked["c"], 2 * g)
                for b in range(PAIR):
                    for c in range(DC):
                        for r in range(4):
                            rows = slice(32 * r, 32 * r + 32)
                            n = (b * DC + c) * N
                            last = pe.matmul(S[:, r, n:n + N], qT[L][rows, c, b * N:(b + 1) * N],
                                             kT[L][rows, c, b * N:(b + 1) * N], start=True, stop=True)
                last.then_inc(s_done[L], 1)

            def tail(L, i, rep):
                stage, other = ("a", "c_tail") if L == "a" else ("c_tail", "a")
                if not runs(stage, rep):
                    return
                g = i - LAG[stage]
                back = 0 if L == "a" else 1

                def turn(b, c):
                    pe.wait_ge(normed[L], 2 * g + b + 1)
                    if b == 1:
                        pe.wait_ge(pT_copied[L][c], 2 * g + 1)
                    elif runs(other, rep - back):
                        M = "c" if L == "a" else "a"
                        pe.wait_ge(pT_copied[M][c], 2 * (i - back - LAG[other] + 1))
                    elif rep - LAG[stage] >= 1:
                        pe.wait_ge(pT_copied[L][c], 2 * g)
                    for r in range(4):
                        last = pe.transpose(PT[c][:, r, :], E[L][:, b, r * DC + c, :], ident[:, :])
                    last.then_inc(pT_done[L][c], 1)

                o = bank(f"pv_{L}", rep)

                def values(b, c):
                    pe.wait_ge(pT_copied[L][c], 2 * g + b + 1)
                    for r in range(4):
                        h = 4 * c + r
                        n = (b * DC + c) * N
                        last = pe.matmul(o[32 * r:32 * r + 32, n:n + N], v[L][:, b, h * HD:(h + 1) * HD],
                                         pT[c][:, r, :], start=True, stop=True)
                    return last

                turn(0, 0)
                turn(0, 1)
                wait_bank(pe, f"pv_{L}", i, rep)
                pe.wait_ge(drained[f"v_{L}"], g + 1)
                values(0, 0)
                turn(1, 0)
                values(0, 1)
                turn(1, 1)
                values(1, 0)
                values(1, 1).then_inc(done[f"pv_{L}"], 1)

                o2 = bank(f"proj_{L}", rep)
                wait_bank(pe, f"proj_{L}", i, rep)
                pe.wait_ge(drained[f"pv_{L}"], g + 1)
                for b in range(PAIR):
                    for c in range(DC):
                        last = pe.matmul(o2[:, b * D:(b + 1) * D], oT[:, b, c, :], wo_sb[L][:, c, :],
                                         start=(c == 0), stop=(c == DC - 1))
                last.then_inc(done[f"proj_{L}"], 1)

            def l1_neighbours(i, rep):
                if not runs("L1", rep):
                    return
                g, p = i - LAG["L1"], (rep - LAG["L1"]) % 2
                o = bank("yT", rep)
                wait_bank(pe, "yT", i, rep)
                pe.wait_ge(x1_made, 2 * (g + 1))
                for b in range(PAIR):
                    for c in range(DC):
                        n = b * DC + c
                        last = pe.matmul(o[:, n * N:(n + 1) * N], x1[:, p, b, c * P:(c + 1) * P], adjT[:, :],
                                         start=True, stop=True)
                last.then_inc(done["yT"], 1)

            def l1_weight(i, rep):
                if not runs("L1", rep):
                    return
                g = i - LAG["L1"]
                o = bank("h1", rep)
                wait_bank(pe, "h1", i, rep)
                pe.wait_ge(drained["yT"], g + 1)
                for b in range(PAIR):
                    for c in range(DC):
                        last = pe.matmul(o[:, b * D:(b + 1) * D], yT[:, b, c, :], w1_sb[:, c, :],
                                         start=(c == 0), stop=(c == DC - 1))
                last.then_inc(done["h1"], 1)

            def l0_product(i, rep):
                if not runs("L0", rep):
                    return
                p = rep % 2
                o = bank("A0", rep)
                wait_bank(pe, "A0", i, rep)
                loads = (i - p) // 2 + 1 if isinstance(i, int) else None
                pe.wait_ge(x_loaded[p], 16 * loads if loads is not None else (i - p) * 8 + 16)
                pe.matmul(o[:, :], adjT[:, :], x0[:, p, :, :], start=True, stop=True).then_inc(done["A0"], 1)

            def body(i, rep):
                project_in("a", i, rep)
                scores("a", i, rep)
                tail("c", i, rep)
                l1_neighbours(i, rep)
                project_in("c", i, rep)
                l1_weight(i, rep)
                scores("c", i, rep)
                l0_product(i, rep)
                tail("a", i, rep)

            engine_program(pe, body)

        @block.scalar
        def _(act):
            act.wait_ge(s_ready, 1)

            def drain_xT(L, i, rep):
                if not runs(L, rep):
                    return
                g = i - LAG[L]
                act.wait_ge(done[f"xT_{L}"], g + 1)
                act.copy(xT[L][:, :, :], bank(f"xT_{L}", rep)[:, :]).then_inc(drained[f"xT_{L}"], 1)

            def drain_k(L, i, rep):
                if not runs(L, rep):
                    return
                g = i - LAG[L]
                o = bank(f"k_{L}", rep)
                act.wait_ge(done[f"k_{L}"], g + 1)
                if L == "a":
                    act.copy(kT[L][:, :, :], o[:, :]).then_inc(drained["k_a"], 1)
                else:
                    for c in range(DC):
                        last = act.activation(kT[L][:, c, :], o[:, c * PAIR * N:(c + 1) * PAIR * N],
                                              ACT.Identity, bias=bk_col[:, c:c + 1])
                    last.then_inc(drained["k_c"], 1)

            def exps(L, b, i, rep):
                stage = "a" if L == "a" else "c_tail"
                if not runs(stage, rep):
                    return
                g = i - LAG[stage]
                act.wait_ge(maxed[L], 2 * g + b + 1)
                if rep - LAG[stage] >= 1:
                    for c in range(2):
                        act.wait_ge(pT_done[L][c], 2 * (g - 1) + b + 1)
                    act.wait_ge(inverted[L], 2 * (g - 1) + b + 1)
                for h in range(HEADS):
                    last = act.activation(E[L][:, b, h, :], t[L][:, b, h, :], ACT.Exp,
                                          bias=nmax[L][:, b, h:h + 1], accum_out=esum[L][:, b, h:h + 1])
                last.then_inc(exped[L], 1)

            def drain_pT(L, b, i, rep):
                stage = "a" if L == "a" else "c_tail"
                if not runs(stage, rep):
                    return
                g = i - LAG[stage]
                act.wait_ge(pT_done[L][0], 2 * g + b + 1)
                act.copy(pT[0][:, :, :], PT[0][:, :, :]).then_inc(pT_copied[L][0], 1)

            def drain_pv(L, i, rep):
                stage = "a" if L == "a" else "c_tail"
                if not runs(stage, rep):
                    return
                g = i - LAG[stage]
                act.wait_ge(done[f"pv_{L}"], g + 1)
                act.copy(oT[:, :, :, :], bank(f"pv_{L}", rep)[:, :]).then_inc(drained[f"pv_{L}"], 1)

            def drain_yT(i, rep):
                if not runs("L1", rep):
                    return
                act.wait_ge(done["yT"], i - LAG["L1"] + 1)
                act.copy(yT[:, :, :, :], bank("yT", rep)[:, :]).then_inc(drained["yT"], 1)

            def add_r0(i, rep):
                if not runs("L0", rep):
                    return
                p = rep % 2
                act.wait_ge(r0_made, i + 1)
                if rep >= 1:
                    act.wait_ge(x1_made, 2 * i)
                for b in range(PAIR):
                    act.activation(t0[:, b, :], x0[:, p, b, :], ACT.Identity,
                                   bias=r0[:, b:b + 1]).then_inc(t0_made, 1)

            def body(i, rep):
                drain_xT("a", i, rep)
                exps("c", 0, i, rep)
                drain_k("a", i, rep)
                exps("c", 1, i, rep)
                drain_pT("c", 0, i, rep)
                drain_pT("c", 1, i, rep)
                drain_pv("c", i, rep)
                drain_yT(i, rep)
                drain_xT("c", i, rep)
                exps("a", 0, i, rep)
                drain_k("c", i, rep)
                exps("a", 1, i, rep)
                add_r0(i, rep)
                drain_pT("a", 0, i, rep)
                drain_pT("a", 1, i, rep)
                drain_pv("a", i, rep)

            engine_program(act, body)

        @block.vector
        def _(dve):
            dve.memset(neg_half[:, :], -0.5)
            dve.memset(ones[:, :], 1.0).then_inc(s_ones, 1)
            dve.wait_ge(s_ones, 1)
            dve.wait_ge(s_w, 16 * N_WEIGHT_DMAS)
            for c in range(DC):
                dve.tensor_scalar(bv_wide[:, c, :], ones[:, :], bv_col[:, c:c + 1], None,
                                  ALU.mult).then_inc(s_setup, 1)
            for n in range(2):
                dve.tensor_scalar(bias["a"][:, n, :], adj_sb[:, :], 0.0, NEG_BIG, ALU.is_equal,
                                  ALU.mult).then_inc(s_setup, 1)
                dve.tensor_scalar(bias["c"][:, n, :], adj_sb[:, :], -1.0, 1.0, ALU.mult,
                                  ALU.add).then_inc(s_setup, 1)
            dve.wait_ge(s_setup, DC + 4)
            dve.tensor_scalar(bias["c"][:, :, :], bias["c"][:, :, :], -1e9, None, ALU.mult).then_inc(s_setup, 1)
            dve.wait_ge(s_adjT, 1)
            dve.tensor_copy(adjT[:, :], GB[0][:, 0:P]).then_inc(s_adjTc, 1)
            dve.wait_ge(s_bvwo, 1)
            dve.tensor_tensor(bo_row[:, :], GB[1][:, 0:D], bo_row[:, :], ALU.add).then_inc(s_setup, 1)
            dve.wait_ge(s_setup, DC + 6)
            dve.wait_ge(s_adjTc, 1)
            dve.memset(mx0[:, :], 0.0).then_inc(s_ready, 1)
            dve.wait_ge(s_ready, 1)

            def statistics(norm, src, g):
                for b in range(PAIR):
                    dve.bn_stats(st[norm][:, b, :], src[:, b, :]).then_inc(stats_made[norm], 1)
                dve.wait_ge(stats_made[norm], 2 * (g + 1))
                dve.memset(gate[:, :], 0.0)
                for b in range(PAIR):
                    dve.bn_aggr(mv[norm][:, b, :], st[norm][:, b, :]).then_inc(aggr_made[norm], 1)
                dve.wait_ge(aggr_made[norm], 2 * (g + 1))
                dve.tensor_scalar(ve[norm][:, :], mv[norm][:, :, 1], LN_EPS, None,
                                  ALU.add).then_inc(var_made[norm], 1)

            def normalise(norm, dst, src, g, made):
                dve.wait_ge(rstd_made[norm], g + 1)
                for b in range(PAIR):
                    dve.tensor_scalar(dst[:, b, :], src[:, b, :], mv[norm][:, b, 0:1], rstd[norm][:, b:b + 1],
                                      ALU.subtract, ALU.mult).then_inc(made, 1)

            def drain_q(L, i, rep):
                if not runs(L, rep):
                    return
                g = i - LAG[L]
                o = bank(f"q_{L}", rep)
                dve.wait_ge(done[f"q_{L}"], g + 1)
                if L == "a":
                    dve.tensor_copy(qT[L][:, :, :], o[:, :]).then_inc(drained["q_a"], 1)
                else:
                    for c in range(DC):
                        last = dve.tensor_scalar(qT[L][:, c, :], o[:, c * PAIR * N:(c + 1) * PAIR * N],
                                                 bq_col[:, c:c + 1], None, ALU.add)
                    last.then_inc(drained["q_c"], 1)

            def drain_v(L, i, rep):
                if not runs(L, rep):
                    return
                g = i - LAG[L]
                dve.wait_ge(done[f"v_{L}"], g + 1)
                dve.tensor_copy(v[L][:, :, :], bank(f"v_{L}", rep)[:, :]).then_inc(drained[f"v_{L}"], 1)

            def mask(L, i, rep):
                if not runs(L, rep):
                    return
                g = i - LAG[L]
                dve.wait_ge(s_done[L], g + 1)
                for b in range(PAIR):
                    if rep - LAG[L] >= 1:
                        dve.wait_ge(exped[L], 2 * (g - 1) + b + 1)
                    dve.scalar_tensor_tensor(
                        out=t[L][:, b, :, :].rearrange("p (r c) n -> p r (c n)", c=DC),
                        in0=S[:, :, b * DC * N:(b + 1) * DC * N], scalar=SCALE,
                        in1=bias[L][:, :, :].rearrange("p c n -> p (c n)").unsqueeze(1)
                            .to_broadcast([P, 4, DC * N]),
                        op0=ALU.mult, op1=ALU.add).then_inc(masked[L], 1)

            def maxima(L, b, i, rep):
                if not runs(L, rep):
                    return
                g = i - LAG[L]
                dve.wait_ge(masked[L], 2 * g + b + 1)
                dve.tensor_reduce(nmax[L][:, b, :], t[L][:, b, :, :], AX_X, ALU.max,
                                  negate=True).then_inc(maxed[L], 1)

            def invert(L, b, i, rep):
                stage = "a" if L == "a" else "c_tail"
                if not runs(stage, rep):
                    return
                g = i - LAG[stage]
                dve.wait_ge(exped[L], 2 * g + b + 1)
                if rep - LAG[stage] >= 1:
                    dve.wait_ge(normed[L], 2 * (g - 1) + b + 1)
                dve.reciprocal(rinv[L][:, b, :], esum[L][:, b, :]).then_inc(inverted[L], 1)

            def drain_pT(L, b, i, rep):
                stage = "a" if L == "a" else "c_tail"
                if not runs(stage, rep):
                    return
                g = i - LAG[stage]
                dve.wait_ge(pT_done[L][1], 2 * g + b + 1)
                dve.tensor_copy(pT[1][:, :, :], PT[1][:, :, :]).then_inc(pT_copied[L][1], 1)

            def l3_residual(i, rep):
                if not runs("c_tail", rep):
                    return
                g, p = i - LAG["c_tail"], (rep - LAG["c_tail"]) % 2
                dve.wait_ge(done["proj_c"], g + 1)
                dve.wait_ge(x3b_made, g + 1)
                if rep - LAG["c_tail"] >= 1:
                    dve.wait_ge(out_made, 2 * g)
                dve.tensor_tensor(h3[:, :, :], bank("proj_c", rep)[:, :], x3b[:, p, :, :],
                                  ALU.add).then_inc(drained["proj_c"], 1)
                dve.wait_ge(drained["proj_c"], g + 1)
                statistics("nc", h3, g)

            def l3_out(i, rep):
                if not runs("c_tail", rep):
                    return
                g, p = i - LAG["c_tail"], (rep - LAG["c_tail"]) % 2
                if rep - LAG["c_tail"] >= 2:
                    dve.wait_ge(stored[p], (g - p) * 8)
                normalise("nc", out_sb[:, p, :, :], h3, g, out_made)

            def l1_residual(i, rep):
                if not runs("L1", rep):
                    return
                g = i - LAG["L1"]
                dve.wait_ge(done["h1"], g + 1)
                dve.wait_ge(x1b_made, g + 1)
                if rep - LAG["L1"] >= 1:
                    dve.wait_ge(x2_made, 2 * g)
                dve.tensor_tensor(h1[:, :, :], bank("h1", rep)[:, :], x1b[:, :, :],
                                  ALU.add).then_inc(drained["h1"], 1)
                dve.wait_ge(drained["h1"], g + 1)
                statistics("n1", h1, g)

            def l1_out(i, rep):
                if not runs("L1", rep):
                    return
                g, p = i - LAG["L1"], (rep - LAG["L1"]) % 2
                if rep - LAG["L1"] >= 2:
                    dve.wait_ge(done["xT_a"], g - 1)
                    dve.wait_ge(x2b_made, g - 1)
                normalise("n1", x2[:, p, :, :], h1, g, x2_made)

            def l0_max(i, rep):
                if not runs("L0", rep):
                    return
                dve.wait_ge(done["A0"], i + 1)
                if rep >= 1:
                    dve.wait_ge(r0_made, i)
                dve.tensor_reduce(mx0[:, :], bank("A0", rep)[:, :].rearrange("p (b n) -> p b n", b=PAIR),
                                  AX_X, ALU.max).then_inc(drained["A0"], 1)
                dve.wait_ge(drained["A0"], i + 1)
                if rep >= 1:
                    dve.wait_ge(t0_made, 2 * i)
                dve.tensor_scalar(r0[:, :], mx0[:, :], b0_col[:, 0:1], 0.0, ALU.add,
                                  ALU.max).then_inc(r0_made, 1)

            def l0_statistics(i, rep):
                if not runs("L0", rep):
                    return
                dve.wait_ge(t0_made, 2 * (i + 1))
                statistics("n0", t0, i)

            def l0_out(i, rep):
                if not runs("L0", rep):
                    return
                p = rep % 2
                if rep >= 2:
                    dve.wait_ge(done["yT"], i - 1)
                    dve.wait_ge(x1b_made, i - 1)
                normalise("n0", x1[:, p, :, :], t0, i, x1_made)

            def l2_bias(i, rep):
                if not runs("a", rep):
                    return
                g = i - LAG["a"]
                dve.wait_ge(done["proj_a"], g + 1)
                if rep - LAG["a"] >= 1:
                    dve.wait_ge(w_made, 2 * g)
                    dve.wait_ge(ox_made, g)
                dve.tensor_tensor(o_sb[:, :, :],
                                  bank("proj_a", rep)[:, :].rearrange("p (b n) -> p b n", b=PAIR),
                                  bp2_row[:, :].unsqueeze(1).to_broadcast([P, PAIR, D]),
                                  ALU.add).then_inc(drained["proj_a"], 1)
                dve.wait_ge(drained["proj_a"], g + 1)
                statistics("ni", o_sb, g)

            def l2_inner(i, rep):
                if not runs("a", rep - 1):
                    return
                g = i - 1 - LAG["a"]
                dve.wait_ge(rstd_made["ni"], g + 1)
                if rep - 1 - LAG["a"] >= 1:
                    dve.wait_ge(h2_made, 2 * g)
                for b in range(PAIR):
                    dve.scalar_tensor_tensor(out=w_ln[:, b, :], in0=o_sb[:, b, :], scalar=mv["ni"][:, b, 0:1],
                                             in1=gam_row[:, :], op0=ALU.subtract,
                                             op1=ALU.mult).then_inc(w_made, 1)
                dve.wait_ge(w_made, 2 * (g + 1))
                dve.wait_ge(ox_made, g + 1)
                if rep - 1 - LAG["a"] >= 1:
                    dve.wait_ge(x3_made, 2 * g)
                for b in range(PAIR):
                    dve.scalar_tensor_tensor(out=h2[:, b, :], in0=w_ln[:, b, :], scalar=rstd["ni"][:, b:b + 1],
                                             in1=ox[:, b, :], op0=ALU.mult, op1=ALU.add).then_inc(h2_made, 1)
                dve.wait_ge(h2_made, 2 * (g + 1))
                statistics("no", h2, g)

            def l2_out(i, rep):
                if not runs("a", rep - 1):
                    return
                g, p = i - 1 - LAG["a"], (rep - 1 - LAG["a"]) % 2
                if rep - 1 - LAG["a"] >= 2:
                    dve.wait_ge(done["xT_c"], g - 1)
                    dve.wait_ge(x3b_made, g - 1)
                normalise("no", x3[:, p, :, :], h2, g, x3_made)

            def body(i, rep):
                l2_inner(i, rep)
                drain_q("a", i, rep)
                invert("c", 0, i, rep)
                drain_v("a", i, rep)
                l2_out(i, rep)
                invert("c", 1, i, rep)
                mask("a", i, rep)
                drain_pT("c", 0, i, rep)
                maxima("a", 0, i, rep)
                drain_pT("c", 1, i, rep)
                maxima("a", 1, i, rep)
                l3_residual(i, rep)
                drain_q("c", i, rep)
                drain_v("c", i, rep)
                invert("a", 0, i, rep)
                l3_out(i, rep)
                l1_residual(i, rep)
                invert("a", 1, i, rep)
                mask("c", i, rep)
                l0_max(i, rep)
                l1_out(i, rep)
                drain_pT("a", 0, i, rep)
                maxima("c", 0, i, rep)
                drain_pT("a", 1, i, rep)
                maxima("c", 1, i, rep)
                l0_statistics(i, rep)
                l2_bias(i, rep)
                l0_out(i, rep)

            engine_program(dve, body)

        @block.gpsimd
        def _(pool):
            pool.memset(ident[:, :], 0.0).then_inc(s_ident, 1)
            pool.wait_ge(s_ident, 1)
            pool.affine_select(out=ident[:, :], in_=ident[:, :], compare_op=ALU.not_equal, fill=1.0,
                               base=0, pattern=[[-1, P]], channel_multiplier=1).then_inc(s_ident, 1)
            pool.wait_ge(s_ready, 1)

            def power(norm, g, had):
                pool.wait_ge(var_made[norm], g + 1)
                pool.tensor_tensor(rstd[norm][:, :], ve[norm][:, :], neg_half[:, :],
                                   ALU.pow).then_inc(rstd_made[norm], 1)

            def normalise(L, b, i, rep):
                stage = "a" if L == "a" else "c_tail"
                if not runs(stage, rep):
                    return
                g = i - LAG[stage]
                pool.wait_ge(inverted[L], 2 * g + b + 1)
                pool.tensor_tensor(E[L][:, b, :, :], E[L][:, b, :, :],
                                   rinv[L][:, b, :].unsqueeze(2).to_broadcast([P, HEADS, N]),
                                   ALU.mult).then_inc(normed[L], 1)

            def add_row(dst, src, row):
                return pool.tensor_tensor(dst, src, row[:, :].unsqueeze(1).to_broadcast([P, PAIR, D]), ALU.add)

            def body(i, rep):
                if runs("a", rep - 1):
                    g, p = i - 1 - LAG["a"], (rep - 1 - LAG["a"]) % 2
                    power("ni", g, rep)
                    pool.wait_ge(drained["proj_a"], g + 1)
                    pool.wait_ge(x2b_made, g + 1)
                    if rep - 1 - LAG["a"] >= 1:
                        pool.wait_ge(h2_made, 2 * g)
                    pool.tensor_tensor(ox[:, :, :], o_sb[:, :, :], x2b[:, p, :, :],
                                       ALU.add).then_inc(ox_made, 1)
                normalise("c", 0, i, rep)
                if runs("a", rep - 1):
                    power("no", g, rep)
                normalise("c", 1, i, rep)
                if runs("a", rep - 1):
                    pool.wait_ge(x3_made, 2 * (g + 1))
                    if rep - 1 - LAG["a"] >= 2:
                        pool.wait_ge(drained["proj_c"], g - 1)
                    add_row(x3b[:, p, :, :], x3[:, p, :, :], bo_row).then_inc(x3b_made, 1)
                if runs("L1", rep):
                    g1, p1 = i - LAG["L1"], (rep - LAG["L1"]) % 2
                    pool.wait_ge(x1_made, 2 * (g1 + 1))
                    if rep - LAG["L1"] >= 1:
                        pool.wait_ge(drained["h1"], g1)
                    add_row(x1b[:, :, :], x1[:, p1, :, :], b1_row).then_inc(x1b_made, 1)
                if runs("c_tail", rep):
                    power("nc", i - LAG["c_tail"], rep)
                normalise("a", 0, i, rep)
                if runs("L1", rep):
                    power("n1", g1, rep)
                normalise("a", 1, i, rep)
                if runs("L1", rep):
                    pool.wait_ge(x2_made, 2 * (g1 + 1))
                    if rep - LAG["L1"] >= 2:
                        pool.wait_ge(ox_made, g1 - 1)
                    add_row(x2b[:, p1, :, :], x2[:, p1, :, :], bet_row).then_inc(x2b_made, 1)
                if runs("L0", rep):
                    power("n0", i, rep)

            engine_program(pool, body)


_INS = ['x', 'adj', 'L0_gnn_b', 'L1_gnn_weight', 'L1_gnn_bias', 'L2_gnn_w_qkv', 'L2_gnn_w_proj',
        'L2_gnn_b_proj', 'L2_gnn_ln_gamma', 'L2_gnn_ln_beta', 'L3_gnn_Wq', 'L3_gnn_bq', 'L3_gnn_Wk',
        'L3_gnn_bk', 'L3_gnn_Wv', 'L3_gnn_bv', 'L3_gnn_Wo', 'L3_gnn_bo']


def kernel(**inputs):
    import numpy as _np
    import concourse.bacc as _bacc
    from concourse import mybir as _mybir
    from concourse.bass_utils import run_bass_kernel_spmd as _run

    nc = _bacc.Bacc("TRN2", target_bir_lowering=False, num_devices=1)
    arrays, args = {}, []
    for name in _INS:
        a = _np.ascontiguousarray(inputs[name])
        arrays[f"in_{name}_dram"] = a
        args.append(nc.dram_tensor(f"in_{name}_dram", a.shape, _mybir.dt.from_np(a.dtype), kind="ExternalInput").ap())
    shape = inputs['x'].shape
    args.append(nc.dram_tensor("out_0_dram", shape, _mybir.dt.float32, kind="ExternalOutput").ap())
    gnn_stack_kernel(nc, *args)
    r = _run(nc, [arrays], core_ids=[0])
    return r.results[0]["out_0_dram"]
```

```python
from contextlib import ExitStack

import concourse.bass as bass
from concourse import mybir

F32 = mybir.dt.float32
F32R = mybir.dt.float32r
ALU = mybir.AluOpType
ACT = mybir.ActivationFunctionType
AX_X = mybir.AxisListType.X

P = 128
PAIR = 2
HEADS = 8
NEG_BIG = -1e30
FAR = 3e38
LN_EPS = 1e-5

LAG = {"L0": 0, "L1": 1, "a": 2, "a_tail": 3, "c": 4, "c_tail": 5}
LAST_LAG = 6

USES = [
    ("yT", "L1", 0), ("pv_c", "c_tail", 1), ("xT_c", "c", 0),
    ("q_c", "c", 0), ("proj_c", "c_tail", 1), ("k_c", "c", 0), ("v_c", "c", 1),
    ("h1", "L1", 0),
    ("A0", "L0", 1), ("pv_a", "a_tail", 0), ("xT_a", "a", 1),
    ("q_a", "a", 1), ("proj_a", "a_tail", 0), ("k_a", "a", 1), ("v_a", "a", 0),
]
NAMES = [u for u, _, _ in USES]


def gnn_stack_kernel(nc, x, adj, b0, w1, b1, wqkv2, wp2, bp2, gam2, bet2,
                     wq3, bq3, wk3, bk3, wv3, bv3, wo3, bo3, out):
    B, N, D = x.shape
    HD = D // HEADS
    DC = D // P
    GROUPS = B // PAIR
    SCALE = float(HD) ** -0.5
    PERIOD = 2
    HEAD_TURNS = 4
    assert N == P and HD == 32 and DC == 2 and GROUPS % PERIOD == 0

    x_v = x.rearrange("(g b) m d -> g m b d", b=PAIR)
    out_v = out.rearrange("(g b) m d -> g m b d", b=PAIR)

    with ExitStack() as ctx:
        def sb(name, shape):
            return ctx.enter_context(nc.sbuf_tensor(name, shape, F32))

        def halves(name, shape):
            return tuple(ctx.enter_context(nc.sbuf_tensor(f"{name}_{half}", shape, F32R))
                         for half in ("upper", "lower"))

        def ps(name, shape):
            return ctx.enter_context(nc.psum_tensor(name, shape, F32))

        def sem(name):
            return ctx.enter_context(nc.semaphore(name))

        ident = sb("ident", [P, P])
        adj_sb = sb("adj_sb", [P, N])
        adjT = sb("adjT", [P, N])
        w_whole = sb("w_whole", [P, DC, 3 * D])
        wo3_sb = sb("wo3_sb", [P, DC, D])
        w1_sb = halves("w1", [P, DC, D])
        wqkv_sb = {L: halves(f"wqkv_{L}", [P, DC, 3 * D]) for L in "ac"}
        wo_sb = {L: halves(f"wo_{L}", [P, DC, D]) for L in "ac"}
        b0_col = sb("b0_col", [P, 1])
        bq_col = sb("bq_col", [P, DC])
        bk_col = sb("bk_col", [P, DC])
        bv_col = sb("bv_col", [P, DC])
        bv_wide = sb("bv_wide", [P, DC, P])
        b1_row = sb("b1_row", [P, D])
        bp2_row = sb("bp2_row", [P, D])
        gam_row = sb("gam_row", [P, D])
        bet_row = sb("bet_row", [P, D])
        bo_row = sb("bo_row", [P, D])
        neg_half = sb("neg_half", [P, PAIR])
        ones = sb("ones", [P, P])
        bias = {"a": sb("bias_a", [P, N]), "c": sb("bias_c", [P, N])}

        x0 = sb("x0", [P, 2, PAIR, D])
        t0 = sb("t0", [P, PAIR, D])
        mx0 = sb("mx0", [P, PAIR])
        r0 = sb("r0", [P, PAIR])
        x1 = sb("x1", [P, 2, PAIR, D])
        x1b = sb("x1b", [P, PAIR, D])
        yT = halves("yT", [P, PAIR, DC, N])
        h1 = sb("h1_sb", [P, PAIR, D])
        x2 = sb("x2", [P, 2, PAIR, D])
        x2b = sb("x2b", [P, 2, PAIR, D])
        o_sb = sb("o_sb", [P, PAIR, D])
        ox = sb("ox", [P, PAIR, D])
        w_ln = sb("w_ln", [P, PAIR, D])
        h2 = sb("h2", [P, PAIR, D])
        x3 = sb("x3", [P, 2, PAIR, D])
        x3b = sb("x3b", [P, 2, PAIR, D])
        h3 = sb("h3", [P, PAIR, D])
        out_sb = sb("out_sb", [P, 2, PAIR, D])
        xin = {"a": x2, "c": x3}

        xT, qT, kT, v, nt, E, nmax, esum, rinv = ({} for _ in range(9))
        for L in "ac":
            xT[L] = halves(f"xT_{L}", [P, DC, PAIR * N])
            qT[L] = sb(f"qT_{L}_sb", [P, DC, PAIR * N])
            kT[L] = sb(f"kT_{L}_sb", [P, DC, PAIR * N])
            v[L] = sb(f"v_{L}_sb", [P, PAIR, D])
            nt[L] = sb(f"nt_{L}_sb", [P, PAIR, HEADS, N])
            E[L] = sb(f"E_{L}_sb", [P, PAIR, HEADS, N])
            nmax[L] = sb(f"nmax_{L}", [P, PAIR, HEADS])
            esum[L] = sb(f"esum_{L}", [P, PAIR, HEADS])
            rinv[L] = sb(f"rinv_{L}", [P, PAIR, HEADS])
        pT = [sb(f"pT_sb{c}", [P, 4, N]) for c in range(2)]
        oT = halves("oT", [P, PAIR, DC, N])
        SPLIT = {"xT_a": xT["a"], "xT_c": xT["c"], "yT": yT, "pv_a": oT, "pv_c": oT}

        gate = sb("gate", [P, 1])
        gate_m = sb("gate_m", [P, 4])
        NORMS = ("n0", "n1", "ni", "no", "nc")
        st = {n: sb(f"st_{n}", [P, PAIR, 6]) for n in NORMS}
        mv = {n: sb(f"mv_{n}", [P, PAIR, 2]) for n in NORMS}
        ve = {n: sb(f"ve_{n}", [P, PAIR]) for n in NORMS}
        rstd = {n: sb(f"rstd_{n}", [P, PAIR]) for n in NORMS}

        S = ps("S", [P, 4, 512])
        PT = [ps(f"PT{c}", [P, 4, N]) for c in range(2)]
        GB = [ps(f"GB{k}", [P, 512]) for k in range(2)]

        s_w = sem("weights_loaded")
        s_ident = sem("ident_made")
        s_ones = sem("ones_made")
        s_setup = sem("setup_vector")
        s_adjT = sem("adjT_done")
        s_adjTc = sem("adjT_copied")
        s_bvwo = sem("bvwo_done")
        s_ready = sem("constants_ready")
        x_loaded = [sem(f"x_loaded{p}") for p in range(2)]
        stored = [sem(f"stored{p}") for p in range(2)]
        done = {u: sem(f"{u}_done") for u in NAMES}
        drained = {u: sem(f"{u}_drained") for u in NAMES}
        upper_made = {u: sem(f"{u}_upper") for u in SPLIT}
        s_wcopied = sem("weight_upper")
        s_wsplit = sem("weight_split")
        s_whole = sem("whole_weight_loaded")
        r0_made = sem("r0_made")
        mx0_made = sem("mx0_made")
        t0_made = sem("t0_made")
        x1_made = sem("x1_made")
        x1b_made = sem("x1b_made")
        x2_made = sem("x2_made")
        x2b_made = sem("x2b_made")
        ox_made = sem("ox_made")
        w_made = sem("w_made")
        h2_made = sem("h2_made")
        x3_made = sem("x3_made")
        x3b_made = sem("x3b_made")
        out_made = sem("out_made")
        xin_made = {"a": x2_made, "c": x3_made}
        s_done = {L: sem(f"scores_{L}_done") for L in "ac"}
        masked, exped, inverted, normed, pT_done, pT_copied = ({} for _ in range(6))
        for L in "ac":
            masked[L] = sem(f"masked_{L}")
            exped[L] = sem(f"exped_{L}")
            inverted[L] = sem(f"inverted_{L}")
            normed[L] = sem(f"normed_{L}")
            pT_done[L] = [sem(f"pT_{L}_done{c}") for c in range(2)]
            pT_copied[L] = [sem(f"pT_{L}_copied{c}") for c in range(2)]
        stats_made = {n: sem(f"stats_{n}") for n in NORMS}
        aggr_made = {n: sem(f"aggr_{n}") for n in NORMS}
        var_made = {n: sem(f"var_{n}") for n in NORMS}
        rstd_made = {n: sem(f"rstd_{n}") for n in NORMS}

        def runs(stage, rep):
            return 0 <= rep - LAG[stage] < GROUPS

        def engine_program(eng, body):
            for i in range(PERIOD * HEAD_TURNS):
                body(i, i)
            with eng.Fori(HEAD_TURNS, GROUPS // PERIOD) as turn:
                for p in range(PERIOD):
                    body(turn * PERIOD + p, PERIOD * HEAD_TURNS + p)
            for i in range(GROUPS, GROUPS + LAST_LAG):
                body(i, i)

        def bank(use):
            return GB[USES[NAMES.index(use)][2]]

        def wait_bank(pe, use, i, rep):
            n = rep * len(USES) + NAMES.index(use)
            for m in range(n - 1, -1, -1):
                before, stage, k = USES[m % len(USES)]
                then = m // len(USES)
                if k == USES[NAMES.index(use)][2] and runs(stage, then):
                    pe.wait_ge(drained[before], i - (rep - then) - LAG[stage] + 1)
                    return

        block = ctx.enter_context(nc.Block())

        def columns(pair, n):
            return tuple(w[:, :, n * D:(n + 1) * D] for w in pair)

        SPLIT_WEIGHTS = [(w1, w1_sb), (wqkv2, wqkv_sb["a"]), (wp2, wo_sb["a"]),
                         (wq3, columns(wqkv_sb["c"], 0)), (wk3, columns(wqkv_sb["c"], 1)),
                         (wv3, columns(wqkv_sb["c"], 2)), (wo3, wo_sb["c"])]

        @block.sync
        def _(sp):
            sp.dma_start(adj_sb[:, :], adj).then_inc(s_w, 16)
            sp.dma_start(wo3_sb[:, :, :], wo3.rearrange("(c p) n -> p c n", p=P)).then_inc(s_w, 16)
            sp.dma_start(b0_col[:, :], b0.rearrange("(p o) -> p o", o=1)).then_inc(s_w, 16)
            for dst, src in ((bq_col, bq3), (bk_col, bk3), (bv_col, bv3)):
                for c in range(DC):
                    sp.dma_start(dst[:, c:c + 1],
                                 src[c * P:(c + 1) * P].rearrange("(p o) -> p o", o=1)).then_inc(s_w, 16)
            for dst, src in ((b1_row, b1), (bp2_row, bp2), (gam_row, gam2), (bet_row, bet2), (bo_row, bo3)):
                sp.dma_start(dst[:, :], src.rearrange("(o n) -> o n", o=1).to_broadcast([P, D])).then_inc(s_w, 16)

            for n, (src, _) in enumerate(SPLIT_WEIGHTS):
                if n >= 1:
                    sp.wait_ge(s_wsplit, n)
                sp.dma_start(w_whole[:, :, 0:src.shape[1]],
                             src.rearrange("(c p) n -> p c n", p=P)).then_inc(s_whole, 16)

            def body(i, rep):
                p = rep % 2
                if runs("L0", rep):
                    g = i
                    if rep >= 2:
                        sp.wait_ge(t0_made, 2 * (g - 1))
                    sp.dma_start(x0[:, p, :, :], x_v[g]).then_inc(x_loaded[p], 16)
                if 0 <= rep - LAST_LAG < GROUPS:
                    g = i - LAST_LAG
                    sp.wait_ge(out_made, 2 * (g + 1))
                    q = (rep - LAST_LAG) % 2
                    sp.dma_start(out_v[g], out_sb[:, q, :, :]).then_inc(stored[q], 16)

            engine_program(sp, body)
            for p in range(2):
                sp.wait_ge(stored[p], 16 * GROUPS // 2)

        N_WEIGHT_DMAS = 1 + 1 + 1 + 3 * DC + 5

        @block.tensor
        def _(pe):
            pe.wait_ge(s_ident, 2)
            pe.wait_ge(s_w, 16 * N_WEIGHT_DMAS)
            pe.transpose(GB[0][:, 0:P], adj_sb[:, :], ident[:, :]).then_inc(s_adjT, 1)
            pe.wait_ge(s_setup, 2)
            for c in range(DC):
                last = pe.matmul(GB[1][:, 0:D], bv_wide[:, c, :], wo3_sb[:, c, :],
                                 start=(c == 0), stop=(c == DC - 1))
            last.then_inc(s_bvwo, 1)
            pe.wait_ge(s_adjTc, 1)
            pe.wait_ge(s_ready, 1)

            def transpose_input(L, i, rep):
                if not runs(L, rep):
                    return
                g, p = i - LAG[L], (rep - LAG[L]) % 2
                o = bank(f"xT_{L}")
                wait_bank(pe, f"xT_{L}", i, rep)
                pe.wait_ge(xin_made[L], 2 * (g + 1))
                for c in range(DC):
                    for b in range(PAIR):
                        n = c * PAIR + b
                        last = pe.transpose(o[:, n * N:(n + 1) * N], xin[L][:, p, b, c * P:(c + 1) * P],
                                            ident[:, :])
                last.then_inc(done[f"xT_{L}"], 1)

            def queries(L, i, rep):
                project_T("q", 0, L, i, rep)

            def keys(L, i, rep):
                project_T("k", 1, L, i, rep)

            def project_T(what, n, L, i, rep):
                if not runs(L, rep):
                    return
                w = columns(wqkv_sb[L], n)
                o = bank(f"{what}_{L}")
                wait_bank(pe, f"{what}_{L}", i, rep)
                g = i - LAG[L]
                pe.wait_ge(upper_made[f"xT_{L}"], g + 1)
                for m in range(DC):
                    for part, (s, x) in enumerate(((0, 0), (1, 0), (0, 1))):
                        if m == 0 and part == 2:
                            pe.wait_ge(drained[f"xT_{L}"], g + 1)
                        for c in range(DC):
                            last = pe.matmul(o[:, m * PAIR * N:(m + 1) * PAIR * N],
                                             w[s][:, c, m * P:(m + 1) * P], xT[L][x][:, c, :],
                                             start=(part == 0 and c == 0), stop=(part == 2 and c == DC - 1))
                last.then_inc(done[f"{what}_{L}"], 1)

            def rows_product(o, data, w, lower, value):
                for b in range(PAIR):
                    for part, (x, s) in enumerate(((0, 0), (0, 1), (1, 0))):
                        if b == 0 and part == 2:
                            pe.wait_ge(lower, value)
                        for c in range(DC):
                            last = pe.matmul(o[:, b * D:(b + 1) * D], data(x, b, c), w[s][:, c, :],
                                             start=(part == 0 and c == 0), stop=(part == 2 and c == DC - 1))
                return last

            def project_v(L, i, rep):
                if not runs(L, rep):
                    return
                wait_bank(pe, f"v_{L}", i, rep)
                rows_product(bank(f"v_{L}"), lambda x, b, c: xT[L][x][:, c, b * N:(b + 1) * N],
                             columns(wqkv_sb[L], 2), drained[f"xT_{L}"],
                             i - LAG[L] + 1).then_inc(done[f"v_{L}"], 1)

            def scores(L, i, rep):
                if not runs(L, rep):
                    return
                g = i - LAG[L]
                pe.wait_ge(drained[f"q_{L}"], g + 1)
                pe.wait_ge(drained[f"k_{L}"], g + 1)
                M, back = ("c", 0) if L == "a" else ("a", 1)
                if runs(M, rep - back):
                    pe.wait_ge(masked[M], 2 * (i - back - LAG[M] + 1))
                elif rep - LAG[L] >= 1:
                    pe.wait_ge(masked[L], 2 * g)
                for b in range(PAIR):
                    for c in range(DC):
                        for r in range(4):
                            rows = slice(32 * r, 32 * r + 32)
                            n = (b * DC + c) * N
                            last = pe.matmul(S[:, r, n:n + N], qT[L][rows, c, b * N:(b + 1) * N],
                                             kT[L][rows, c, b * N:(b + 1) * N], start=True, stop=True)
                last.then_inc(s_done[L], 1)

            def turn(L, b, c, i, rep):
                stage = f"{L}_tail"
                if not runs(stage, rep):
                    return
                g = i - LAG[stage]
                pe.wait_ge(normed[L], 2 * g + b + 1)
                M, back = ("c", 0) if L == "a" else ("a", 1)
                if b == 1:
                    pe.wait_ge(pT_copied[L][c], 2 * g + 1)
                elif runs(f"{M}_tail", rep - back):
                    pe.wait_ge(pT_copied[M][c], 2 * (i - back - LAG[f"{M}_tail"] + 1))
                elif rep - LAG[stage] >= 1:
                    pe.wait_ge(pT_copied[L][c], 2 * g)
                for r in range(4):
                    last = pe.transpose(PT[c][:, r, :], E[L][:, b, r * DC + c, :], ident[:, :])
                last.then_inc(pT_done[L][c], 1)

            def values(L, b, c, i, rep):
                stage = f"{L}_tail"
                if not runs(stage, rep):
                    return
                g = i - LAG[stage]
                if (b, c) == (0, 0):
                    wait_bank(pe, f"pv_{L}", i, rep)
                    pe.wait_ge(drained[f"v_{L}"], g + 1)
                pe.wait_ge(pT_copied[L][c], 2 * g + b + 1)
                o = bank(f"pv_{L}")
                for r in range(4):
                    h = 4 * c + r
                    n = (b * DC + c) * N
                    last = pe.matmul(o[32 * r:32 * r + 32, n:n + N], v[L][:, b, h * HD:(h + 1) * HD],
                                     pT[c][:, r, :], start=True, stop=True)
                if (b, c) == (PAIR - 1, DC - 1):
                    last.then_inc(done[f"pv_{L}"], 1)

            def project_out(L, i, rep):
                stage = f"{L}_tail"
                if not runs(stage, rep):
                    return
                g = i - LAG[stage]
                wait_bank(pe, f"proj_{L}", i, rep)
                pe.wait_ge(upper_made[f"pv_{L}"], g + 1)
                rows_product(bank(f"proj_{L}"), lambda x, b, c: oT[x][:, b, c, :], wo_sb[L],
                             drained[f"pv_{L}"], g + 1).then_inc(done[f"proj_{L}"], 1)

            def l1_neighbours(i, rep):
                if not runs("L1", rep):
                    return
                g, p = i - LAG["L1"], (rep - LAG["L1"]) % 2
                o = bank("yT")
                wait_bank(pe, "yT", i, rep)
                pe.wait_ge(x1_made, 2 * (g + 1))
                for b in range(PAIR):
                    for c in range(DC):
                        n = b * DC + c
                        last = pe.matmul(o[:, n * N:(n + 1) * N], x1[:, p, b, c * P:(c + 1) * P], adjT[:, :],
                                         start=True, stop=True)
                last.then_inc(done["yT"], 1)

            def l1_weight(i, rep):
                if not runs("L1", rep):
                    return
                g = i - LAG["L1"]
                wait_bank(pe, "h1", i, rep)
                pe.wait_ge(upper_made["yT"], g + 1)
                rows_product(bank("h1"), lambda x, b, c: yT[x][:, b, c, :], w1_sb,
                             drained["yT"], g + 1).then_inc(done["h1"], 1)

            def l0_product(i, rep):
                if not runs("L0", rep):
                    return
                p = rep % 2
                o = bank("A0")
                wait_bank(pe, "A0", i, rep)
                loads = (i - p) // 2 + 1 if isinstance(i, int) else None
                pe.wait_ge(x_loaded[p], 16 * loads if loads is not None else (i - p) * 8 + 16)
                pe.matmul(o[:, :], adjT[:, :], x0[:, p, :, :], start=True, stop=True).then_inc(done["A0"], 1)

            def body(i, rep):
                for L, filler in (("c", l1_neighbours), ("a", l0_product)):
                    turn(L, 0, 0, i, rep)
                    turn(L, 0, 1, i, rep)
                    filler(i, rep)
                    values(L, 0, 0, i, rep)
                    turn(L, 1, 0, i, rep)
                    values(L, 0, 1, i, rep)
                    transpose_input(L, i, rep)
                    turn(L, 1, 1, i, rep)
                    values(L, 1, 0, i, rep)
                    values(L, 1, 1, i, rep)
                    queries(L, i, rep)
                    project_out(L, i, rep)
                    keys(L, i, rep)
                    project_v(L, i, rep)
                    if L == "c":
                        l1_weight(i, rep)
                    scores(L, i, rep)

            engine_program(pe, body)

        @block.scalar
        def _(act):
            for n, (src, dst) in enumerate(SPLIT_WEIGHTS):
                act.wait_ge(s_whole, 16 * (n + 1))
                act.copy(dst[0][:, :, :], w_whole[:, :, 0:src.shape[1]]).then_inc(s_wcopied, 1)
            act.wait_ge(s_ready, 1)

            def upper_half(use, stage, i, rep):
                if not runs(stage, rep):
                    return
                g = i - LAG[stage]
                act.wait_ge(done[use], g + 1)
                dst = SPLIT[use][0]
                act.copy(dst[:, :, :] if len(dst.shape) == 3 else dst[:, :, :, :],
                         bank(use)[:, :]).then_inc(upper_made[use], 1)

            def drain_k(L, i, rep):
                if not runs(L, rep):
                    return
                g = i - LAG[L]
                o = bank(f"k_{L}")
                act.wait_ge(done[f"k_{L}"], g + 1)
                if L == "a":
                    act.copy(kT[L][:, :, :], o[:, :]).then_inc(drained["k_a"], 1)
                else:
                    for c in range(DC):
                        last = act.activation(kT[L][:, c, :], o[:, c * PAIR * N:(c + 1) * PAIR * N],
                                              ACT.Identity, bias=bk_col[:, c:c + 1])
                    last.then_inc(drained["k_c"], 1)

            def exps(L, b, stage, i, rep):
                if not runs(stage, rep):
                    return
                g = i - LAG[stage]
                act.wait_ge(masked[L], 2 * g + b + 1)
                if rep - LAG[stage] >= 1:
                    for c in range(2):
                        act.wait_ge(pT_done[L][c], 2 * (g - 1) + b + 1)
                    act.wait_ge(inverted[L], 2 * (g - 1) + b + 1)
                for h in range(HEADS):
                    last = act.activation(E[L][:, b, h, :], nt[L][:, b, h, :], ACT.Exp, scale=-1.0,
                                          bias=nmax[L][:, b, h:h + 1], accum_out=esum[L][:, b, h:h + 1])
                last.then_inc(exped[L], 1)

            def drain_pT(L, b, c, i, rep):
                stage = f"{L}_tail"
                if not runs(stage, rep):
                    return
                g = i - LAG[stage]
                act.wait_ge(pT_done[L][c], 2 * g + b + 1)
                act.copy(pT[c][:, :, :], PT[c][:, :, :]).then_inc(pT_copied[L][c], 1)

            def add_r0(i, rep):
                if not runs("L0", rep):
                    return
                p = rep % 2
                act.wait_ge(r0_made, i + 1)
                if rep >= 1:
                    act.wait_ge(x1_made, 2 * i)
                for b in range(PAIR):
                    act.activation(t0[:, b, :], x0[:, p, b, :], ACT.Identity,
                                   bias=r0[:, b:b + 1]).then_inc(t0_made, 1)

            def body(i, rep):
                for L in "ca":
                    drain_pT(L, 0, 0, i, rep)
                    drain_pT(L, 0, 1, i, rep)
                    if L == "c":
                        upper_half("yT", "L1", i, rep)
                    drain_pT(L, 1, 0, i, rep)
                    upper_half(f"xT_{L}", L, i, rep)
                    drain_pT(L, 1, 1, i, rep)
                    upper_half(f"pv_{L}", f"{L}_tail", i, rep)
                    M, stage = ("a", "a_tail") if L == "c" else ("c", "c")
                    exps(M, 0, stage, i, rep)
                    if L == "a":
                        add_r0(i, rep)
                    drain_k(L, i, rep)
                    exps(M, 1, stage, i, rep)

            engine_program(act, body)

        @block.vector
        def _(dve):
            dve.memset(neg_half[:, :], -0.5)
            dve.memset(ones[:, :], 1.0).then_inc(s_ones, 1)
            dve.wait_ge(s_ones, 1)
            dve.wait_ge(s_w, 16 * N_WEIGHT_DMAS)
            for c in range(DC):
                dve.tensor_scalar(bv_wide[:, c, :], ones[:, :], bv_col[:, c:c + 1], None,
                                  ALU.mult).then_inc(s_setup, 1)
            dve.tensor_scalar(bias["a"][:, :], adj_sb[:, :], 0.0, NEG_BIG, ALU.is_equal,
                              ALU.mult).then_inc(s_setup, 1)
            dve.tensor_scalar(bias["c"][:, :], adj_sb[:, :], -1.0, 1.0, ALU.mult, ALU.add).then_inc(s_setup, 1)
            dve.wait_ge(s_setup, DC + 2)
            dve.tensor_scalar(bias["c"][:, :], bias["c"][:, :], -1e9, None, ALU.mult).then_inc(s_setup, 1)
            for n, (src, dst) in enumerate(SPLIT_WEIGHTS):
                dve.wait_ge(s_wcopied, n + 1)
                dve.tensor_tensor(dst[1][:, :, :], w_whole[:, :, 0:src.shape[1]],
                                  dst[0][:, :, :].bitcast(F32), ALU.subtract).then_inc(s_wsplit, 1)
            dve.wait_ge(s_adjT, 1)
            dve.tensor_copy(adjT[:, :], GB[0][:, 0:P]).then_inc(s_adjTc, 1)
            dve.wait_ge(s_bvwo, 1)
            dve.tensor_tensor(bo_row[:, :], GB[1][:, 0:D], bo_row[:, :], ALU.add).then_inc(s_setup, 1)
            dve.wait_ge(s_setup, DC + 4)
            dve.wait_ge(s_adjTc, 1)
            dve.wait_ge(s_wsplit, len(SPLIT_WEIGHTS))
            dve.memset(mx0[:, :], 0.0).then_inc(s_ready, 1)
            dve.wait_ge(s_ready, 1)

            def statistics(norm, src, g):
                for b in range(PAIR):
                    dve.bn_stats(st[norm][:, b, :], src[:, b, :]).then_inc(stats_made[norm], 1)
                dve.wait_ge(stats_made[norm], 2 * (g + 1))
                dve.memset(gate[:, :], 0.0)
                for b in range(PAIR):
                    dve.bn_aggr(mv[norm][:, b, :], st[norm][:, b, :]).then_inc(aggr_made[norm], 1)
                dve.wait_ge(aggr_made[norm], 2 * (g + 1))
                dve.tensor_scalar(ve[norm][:, :], mv[norm][:, :, 1], LN_EPS, None,
                                  ALU.add).then_inc(var_made[norm], 1)

            def normalise(norm, dst, src, g, made):
                dve.wait_ge(rstd_made[norm], g + 1)
                for b in range(PAIR):
                    dve.tensor_scalar(dst[:, b, :], src[:, b, :], mv[norm][:, b, 0:1], rstd[norm][:, b:b + 1],
                                      ALU.subtract, ALU.mult).then_inc(made, 1)

            def lower_half(use, stage, i, rep):
                if not runs(stage, rep):
                    return
                g = i - LAG[stage]
                dve.wait_ge(upper_made[use], g + 1)
                upper, lower = SPLIT[use]
                every = (slice(None),) * len(upper.shape)
                dve.tensor_tensor(lower[every], bank(use)[:, :], upper[every].bitcast(F32),
                                  ALU.subtract).then_inc(drained[use], 1)

            def drain_q(L, i, rep):
                if not runs(L, rep):
                    return
                g = i - LAG[L]
                o = bank(f"q_{L}")
                dve.wait_ge(done[f"q_{L}"], g + 1)
                if L == "a":
                    dve.tensor_scalar(qT[L][:, :, :], o[:, :], SCALE, None, ALU.mult).then_inc(drained["q_a"], 1)
                else:
                    for c in range(DC):
                        last = dve.tensor_scalar(qT[L][:, c, :], o[:, c * PAIR * N:(c + 1) * PAIR * N],
                                                 bq_col[:, c:c + 1], SCALE, ALU.add, ALU.mult)
                    last.then_inc(drained["q_c"], 1)

            def drain_v(L, i, rep):
                if not runs(L, rep):
                    return
                g = i - LAG[L]
                dve.wait_ge(done[f"v_{L}"], g + 1)
                dve.tensor_copy(v[L][:, :, :], bank(f"v_{L}")[:, :]).then_inc(drained[f"v_{L}"], 1)

            def mask(L, b, stage, i, rep):
                if not runs(stage, rep):
                    return
                g = i - LAG[stage]
                dve.wait_ge(s_done[L], g + 1)
                if rep - LAG[stage] >= 1:
                    dve.wait_ge(exped[L], 2 * (g - 1) + b + 1)
                at = "ac".index(L) * PAIR + b
                dve.memset(gate_m[:, at:at + 1], 0.0)
                for r in range(4):
                    for c in range(DC):
                        h, n = r * DC + c, (b * DC + c) * N
                        last = dve.tensor_tensor_reduce(nt[L][:, b, h, :], S[:, r, n:n + N], bias[L][:, :],
                                                        -1.0, FAR, ALU.add, ALU.min, nmax[L][:, b, h:h + 1])
                last.then_inc(masked[L], 1)

            def invert(L, b, stage, i, rep):
                if not runs(stage, rep):
                    return
                g = i - LAG[stage]
                dve.wait_ge(exped[L], 2 * g + b + 1)
                if rep - LAG[stage] >= 1:
                    dve.wait_ge(normed[L], 2 * (g - 1) + b + 1)
                dve.reciprocal(rinv[L][:, b, :], esum[L][:, b, :]).then_inc(inverted[L], 1)

            def l3_residual(i, rep):
                if not runs("c_tail", rep):
                    return
                g, p = i - LAG["c_tail"], (rep - LAG["c_tail"]) % 2
                dve.wait_ge(done["proj_c"], g + 1)
                dve.wait_ge(x3b_made, g + 1)
                if rep - LAG["c_tail"] >= 1:
                    dve.wait_ge(out_made, 2 * g)
                dve.tensor_tensor(h3[:, :, :], bank("proj_c")[:, :], x3b[:, p, :, :],
                                  ALU.add).then_inc(drained["proj_c"], 1)
                dve.wait_ge(drained["proj_c"], g + 1)
                statistics("nc", h3, g)

            def l3_out(i, rep):
                if not runs("c_tail", rep):
                    return
                g, p = i - LAG["c_tail"], (rep - LAG["c_tail"]) % 2
                if rep - LAG["c_tail"] >= 2:
                    dve.wait_ge(stored[p], (g - p) * 8)
                normalise("nc", out_sb[:, p, :, :], h3, g, out_made)

            def l1_residual(i, rep):
                if not runs("L1", rep):
                    return
                g = i - LAG["L1"]
                dve.wait_ge(done["h1"], g + 1)
                dve.wait_ge(x1b_made, g + 1)
                if rep - LAG["L1"] >= 1:
                    dve.wait_ge(x2_made, 2 * g)
                dve.tensor_tensor(h1[:, :, :], bank("h1")[:, :], x1b[:, :, :],
                                  ALU.add).then_inc(drained["h1"], 1)
                dve.wait_ge(drained["h1"], g + 1)
                statistics("n1", h1, g)

            def l1_out(i, rep):
                if not runs("L1", rep):
                    return
                g, p = i - LAG["L1"], (rep - LAG["L1"]) % 2
                if rep - LAG["L1"] >= 2:
                    dve.wait_ge(done["xT_a"], g - 1)
                    dve.wait_ge(x2b_made, g - 1)
                normalise("n1", x2[:, p, :, :], h1, g, x2_made)

            def l0_max(i, rep):
                if not runs("L0", rep):
                    return
                dve.wait_ge(done["A0"], i + 1)
                if rep >= 1:
                    dve.wait_ge(r0_made, i)
                dve.tensor_reduce(mx0[:, :], bank("A0")[:, :].rearrange("p (b n) -> p b n", b=PAIR),
                                  AX_X, ALU.max).then_inc(drained["A0"], 1)
                dve.wait_ge(drained["A0"], i + 1)
                if rep >= 1:
                    dve.wait_ge(t0_made, 2 * i)
                dve.tensor_scalar(r0[:, :], mx0[:, :], b0_col[:, 0:1], 0.0, ALU.add,
                                  ALU.max).then_inc(r0_made, 1)

            def l0_statistics(i, rep):
                if not runs("L0", rep):
                    return
                dve.wait_ge(t0_made, 2 * (i + 1))
                statistics("n0", t0, i)

            def l0_out(i, rep):
                if not runs("L0", rep):
                    return
                p = rep % 2
                if rep >= 2:
                    dve.wait_ge(done["yT"], i - 1)
                    dve.wait_ge(x1b_made, i - 1)
                normalise("n0", x1[:, p, :, :], t0, i, x1_made)

            def l2_bias(i, rep):
                if not runs("a_tail", rep):
                    return
                g = i - LAG["a_tail"]
                dve.wait_ge(done["proj_a"], g + 1)
                if rep - LAG["a_tail"] >= 1:
                    dve.wait_ge(w_made, 2 * g)
                    dve.wait_ge(ox_made, g)
                dve.tensor_tensor(o_sb[:, :, :],
                                  bank("proj_a")[:, :].rearrange("p (b n) -> p b n", b=PAIR),
                                  bp2_row[:, :].unsqueeze(1).to_broadcast([P, PAIR, D]),
                                  ALU.add).then_inc(drained["proj_a"], 1)
                dve.wait_ge(drained["proj_a"], g + 1)
                statistics("ni", o_sb, g)

            def l2_inner(i, rep):
                if not runs("a_tail", rep):
                    return
                g = i - LAG["a_tail"]
                dve.wait_ge(rstd_made["ni"], g + 1)
                if rep - LAG["a_tail"] >= 1:
                    dve.wait_ge(h2_made, 2 * g)
                for b in range(PAIR):
                    dve.scalar_tensor_tensor(out=w_ln[:, b, :], in0=o_sb[:, b, :], scalar=mv["ni"][:, b, 0:1],
                                             in1=gam_row[:, :], op0=ALU.subtract,
                                             op1=ALU.mult).then_inc(w_made, 1)
                dve.wait_ge(w_made, 2 * (g + 1))
                dve.wait_ge(ox_made, g + 1)
                if rep - LAG["a_tail"] >= 1:
                    dve.wait_ge(x3_made, 2 * g)
                for b in range(PAIR):
                    dve.scalar_tensor_tensor(out=h2[:, b, :], in0=w_ln[:, b, :], scalar=rstd["ni"][:, b:b + 1],
                                             in1=ox[:, b, :], op0=ALU.mult, op1=ALU.add).then_inc(h2_made, 1)
                dve.wait_ge(h2_made, 2 * (g + 1))
                statistics("no", h2, g)

            def l2_out(i, rep):
                if not runs("a_tail", rep):
                    return
                g, p = i - LAG["a_tail"], (rep - LAG["a_tail"]) % 2
                if rep - LAG["a_tail"] >= 2:
                    dve.wait_ge(done["xT_c"], g - 1)
                    dve.wait_ge(x3b_made, g - 1)
                normalise("no", x3[:, p, :, :], h2, g, x3_made)

            def body(i, rep):
                mask("a", 0, "a_tail", i, rep)
                lower_half("yT", "L1", i, rep)
                mask("a", 1, "a_tail", i, rep)
                lower_half("xT_c", "c", i, rep)
                lower_half("pv_c", "c_tail", i, rep)
                drain_q("c", i, rep)
                l3_residual(i, rep)
                invert("a", 0, "a_tail", i, rep)
                drain_v("c", i, rep)
                l1_residual(i, rep)
                l3_out(i, rep)
                invert("a", 1, "a_tail", i, rep)
                l1_out(i, rep)
                mask("c", 0, "c", i, rep)
                l0_max(i, rep)
                mask("c", 1, "c", i, rep)
                lower_half("xT_a", "a", i, rep)
                lower_half("pv_a", "a_tail", i, rep)
                drain_q("a", i, rep)
                invert("c", 0, "c", i, rep)
                l2_bias(i, rep)
                l0_statistics(i, rep)
                l2_inner(i, rep)
                drain_v("a", i, rep)
                l0_out(i, rep)
                l2_out(i, rep)
                invert("c", 1, "c", i, rep)

            engine_program(dve, body)

        @block.gpsimd
        def _(pool):
            pool.memset(ident[:, :], 0.0).then_inc(s_ident, 1)
            pool.wait_ge(s_ident, 1)
            pool.affine_select(out=ident[:, :], in_=ident[:, :], compare_op=ALU.not_equal, fill=1.0,
                               base=0, pattern=[[-1, P]], channel_multiplier=1).then_inc(s_ident, 1)
            pool.wait_ge(s_ready, 1)

            def normalise(L, b, stage, i, rep):
                if not runs(stage, rep):
                    return
                pool.wait_ge(inverted[L], 2 * (i - LAG[stage]) + b + 1)
                pool.tensor_tensor(E[L][:, b, :, :], E[L][:, b, :, :],
                                   rinv[L][:, b, :].unsqueeze(2).to_broadcast([P, HEADS, N]),
                                   ALU.mult).then_inc(normed[L], 1)

            def add_row(dst, src, row):
                return pool.tensor_tensor(dst, src, row[:, :].unsqueeze(1).to_broadcast([P, PAIR, D]), ALU.add)

            def power(norm, stage, i, rep):
                if not runs(stage, rep):
                    return
                g = i - LAG[stage]
                pool.wait_ge(var_made[norm], g + 1)
                pool.tensor_tensor(rstd[norm][:, :], ve[norm][:, :], neg_half[:, :],
                                   ALU.pow).then_inc(rstd_made[norm], 1)

            def add_b1(i, rep):
                if not runs("L1", rep):
                    return
                g, p = i - LAG["L1"], (rep - LAG["L1"]) % 2
                pool.wait_ge(x1_made, 2 * (g + 1))
                if rep - LAG["L1"] >= 1:
                    pool.wait_ge(drained["h1"], g)
                add_row(x1b[:, :, :], x1[:, p, :, :], b1_row).then_inc(x1b_made, 1)

            def add_beta(i, rep):
                if not runs("a", rep):
                    return
                g, p = i - LAG["a"], (rep - LAG["a"]) % 2
                pool.wait_ge(x2_made, 2 * (g + 1))
                if rep - LAG["a"] >= 2:
                    pool.wait_ge(ox_made, g - 1)
                add_row(x2b[:, p, :, :], x2[:, p, :, :], bet_row).then_inc(x2b_made, 1)

            def add_bo(i, rep):
                if not runs("c", rep):
                    return
                g, p = i - LAG["c"], (rep - LAG["c"]) % 2
                pool.wait_ge(x3_made, 2 * (g + 1))
                if rep - LAG["c"] >= 2:
                    pool.wait_ge(drained["proj_c"], g - 1)
                add_row(x3b[:, p, :, :], x3[:, p, :, :], bo_row).then_inc(x3b_made, 1)

            def add_o(i, rep):
                if not runs("a_tail", rep):
                    return
                g, p = i - LAG["a_tail"], (rep - LAG["a_tail"]) % 2
                pool.wait_ge(drained["proj_a"], g + 1)
                pool.wait_ge(x2b_made, g + 1)
                if rep - LAG["a_tail"] >= 1:
                    pool.wait_ge(h2_made, 2 * g)
                pool.tensor_tensor(ox[:, :, :], o_sb[:, :, :], x2b[:, p, :, :], ALU.add).then_inc(ox_made, 1)

            def body(i, rep):
                add_bo(i, rep)
                add_b1(i, rep)
                add_beta(i, rep)
                power("nc", "c_tail", i, rep)
                normalise("a", 0, "a_tail", i, rep)
                power("n1", "L1", i, rep)
                normalise("a", 1, "a_tail", i, rep)
                power("ni", "a_tail", i, rep)
                add_o(i, rep)
                normalise("c", 0, "c", i, rep)
                power("no", "a_tail", i, rep)
                power("n0", "L0", i, rep)
                normalise("c", 1, "c", i, rep)

            engine_program(pool, body)


_INS = ['x', 'adj', 'L0_gnn_b', 'L1_gnn_weight', 'L1_gnn_bias', 'L2_gnn_w_qkv', 'L2_gnn_w_proj',
        'L2_gnn_b_proj', 'L2_gnn_ln_gamma', 'L2_gnn_ln_beta', 'L3_gnn_Wq', 'L3_gnn_bq', 'L3_gnn_Wk',
        'L3_gnn_bk', 'L3_gnn_Wv', 'L3_gnn_bv', 'L3_gnn_Wo', 'L3_gnn_bo']


def kernel(**inputs):
    import numpy as _np
    import concourse.bacc as _bacc
    from concourse import mybir as _mybir
    from concourse.bass_utils import run_bass_kernel_spmd as _run

    nc = _bacc.Bacc("TRN2", target_bir_lowering=False, num_devices=1)
    arrays, args = {}, []
    for name in _INS:
        a = _np.ascontiguousarray(inputs[name])
        arrays[f"in_{name}_dram"] = a
        args.append(nc.dram_tensor(f"in_{name}_dram", a.shape, _mybir.dt.from_np(a.dtype), kind="ExternalInput").ap())
    shape = inputs['x'].shape
    args.append(nc.dram_tensor("out_0_dram", shape, _mybir.dt.float32, kind="ExternalOutput").ap())
    gnn_stack_kernel(nc, *args)
    r = _run(nc, [arrays], core_ids=[0])
    return r.results[0]["out_0_dram"]
```

```python
from contextlib import ExitStack

from concourse import mybir

F32 = mybir.dt.float32
F32R = mybir.dt.float32r
ALU = mybir.AluOpType
ACT = mybir.ActivationFunctionType
AX_X = mybir.AxisListType.X

P = 128
PAIR = 2
HEADS = 8
UNITS = 2
UNIT_HEADS = PAIR * HEADS // UNITS
NEG_BIG = -1e30
FAR = 3e38
LN_EPS = 1e-5

LAG = {"L0": 0, "L1": 1, "a": 2, "a_tail": 3, "a_out": 4, "c": 5, "c_tail": 6}
LAST_LAG = 7

USES = [
    ("yT", "L1", 0), ("pv_c", "c_tail", 1), ("xT_c", "c", 0),
    ("q_c", "c", 0), ("k_c", "c", 1), ("proj_c", "c_tail", 0), ("v_c", "c", 1),
    ("h1", "L1", 0),
    ("A0", "L0", 1), ("pv_a", "a_tail", 0), ("xT_a", "a", 1),
    ("q_a", "a", 1), ("k_a", "a", 0), ("proj_a", "a_tail", 1), ("v_a", "a", 0),
]
NAMES = [u for u, _, _ in USES]


def gnn_stack_kernel(nc, x, adj, b0, w1, b1, wqkv2, wp2, bp2, gam2, bet2,
                     wq3, bq3, wk3, bk3, wv3, bv3, wo3, bo3, out):
    B, N, D = x.shape
    HD = D // HEADS
    DC = D // P
    GROUPS = B // PAIR
    SCALE = float(HD) ** -0.5
    PERIOD = 2
    HEAD_TURNS = 4
    assert N == P and HD == 32 and DC == 2 and GROUPS % PERIOD == 0

    x_v = x.rearrange("(g b) m d -> g m b d", b=PAIR)
    out_v = out.rearrange("(g b) m d -> g m b d", b=PAIR)

    with ExitStack() as ctx:
        def sb(name, shape):
            return ctx.enter_context(nc.sbuf_tensor(name, shape, F32))

        def halves(name, shape):
            return tuple(ctx.enter_context(nc.sbuf_tensor(f"{name}_{half}", shape, F32R))
                         for half in ("upper", "lower"))

        def ps(name, shape):
            return ctx.enter_context(nc.psum_tensor(name, shape, F32))

        def sem(name):
            return ctx.enter_context(nc.semaphore(name))

        ident = sb("ident", [P, P])
        adj_sb = sb("adj_sb", [P, N])
        adjT = sb("adjT", [P, N])
        adjT_h = halves("adjT", [P, N])
        w1_sb = halves("w1", [P, DC, D])
        wqkv_sb = {L: halves(f"wqkv_{L}", [P, DC, 3 * D]) for L in "ac"}
        wo_sb = {L: halves(f"wo_{L}", [P, DC, D]) for L in "ac"}
        b0_col = sb("b0_col", [P, 1])
        bq_col = sb("bq_col", [P, DC])
        bk_col = sb("bk_col", [P, DC])
        bv_col = sb("bv_col", [P, DC])
        bv_wide = sb("bv_wide", [P, DC, P])
        b1_row = sb("b1_row", [P, D])
        bp2_row = sb("bp2_row", [P, D])
        gam_row = sb("gam_row", [P, D])
        bet_row = sb("bet_row", [P, D])
        bo_row = sb("bo_row", [P, D])
        neg_half = sb("neg_half", [P, PAIR])
        ones = sb("ones", [P, P])
        bias = {"a": sb("bias_a", [P, N]), "c": sb("bias_c", [P, N])}

        x0 = sb("x0", [P, 2, PAIR, D])
        x0_h = halves("x0", [P, PAIR, D])
        t0 = sb("t0", [P, PAIR, D])
        mx0 = sb("mx0", [P, PAIR])
        r0 = sb("r0", [P, PAIR])
        x1 = sb("x1", [P, 2, PAIR, D])
        x1b = sb("x1b", [P, PAIR, D])
        yT = halves("yT", [P, PAIR, DC, N])
        h1 = sb("h1_sb", [P, PAIR, D])
        x2 = sb("x2", [P, 2, PAIR, D])
        x2b = sb("x2b", [P, 2, PAIR, D])
        o_sb = sb("o_sb", [P, PAIR, D])
        ox = sb("ox", [P, PAIR, D])
        w_ln = sb("w_ln", [P, PAIR, D])
        h2 = sb("h2", [P, PAIR, D])
        x3 = sb("x3", [P, 2, PAIR, D])
        x3b = sb("x3b", [P, 2, PAIR, D])
        h3 = sb("h3", [P, PAIR, D])
        out_sb = sb("out_sb", [P, 2, PAIR, D])
        xin = {"a": x2, "c": x3}

        xT, qT, kT, v, nt, E, nmax, esum, rinv = ({} for _ in range(9))
        for L in "ac":
            xT[L] = halves(f"xT_{L}", [P, DC, PAIR * N])
            qT[L] = sb(f"qT_{L}_sb", [P, DC, PAIR * N])
            kT[L] = sb(f"kT_{L}_sb", [P, DC, PAIR * N])
            v[L] = sb(f"v_{L}_sb", [P, PAIR, D])
            nt[L] = sb(f"nt_{L}_sb", [P, UNITS, UNIT_HEADS, N])
            E[L] = sb(f"E_{L}_sb", [P, UNITS, UNIT_HEADS, N])
            nmax[L] = sb(f"nmax_{L}", [P, UNITS, UNIT_HEADS])
            esum[L] = sb(f"esum_{L}", [P, UNITS, UNIT_HEADS])
            rinv[L] = sb(f"rinv_{L}", [P, UNITS, UNIT_HEADS])
        pT = [[sb(f"pT_sb{u}{b}", [P, 4, N]) for b in range(PAIR)] for u in range(UNITS)]
        oT = halves("oT", [P, PAIR, DC, N])
        SPLIT = {"xT_a": xT["a"], "xT_c": xT["c"], "yT": yT, "pv_a": oT, "pv_c": oT}

        gate = sb("gate", [P, 1])
        gate_m = sb("gate_m", [P, 4])
        NORMS = ("n0", "n1", "ni", "no", "nc")
        st = {n: sb(f"st_{n}", [P, PAIR, 6]) for n in NORMS}
        mv = {n: sb(f"mv_{n}", [P, PAIR, 2]) for n in NORMS}
        ve = {n: sb(f"ve_{n}", [P, PAIR]) for n in NORMS}
        rstd = {n: sb(f"rstd_{n}", [P, PAIR]) for n in NORMS}

        S = ps("S", [P, 4, 512])
        PT = [ps(f"PT{b}", [P, 4, N]) for b in range(PAIR)]
        GB = [ps(f"GB{k}", [P, 512]) for k in range(2)]

        s_adj = sem("adj_loaded")
        s_b0 = sem("b0_loaded")
        s_small = sem("small_constants_loaded")
        s_ident = sem("ident_made")
        s_ones = sem("ones_made")
        s_half = sem("neg_half_made")
        s_setup = sem("setup_vector")
        s_adjT = sem("adjT_done")
        s_adjTc = sem("adjT_copied")
        s_bvwo = sem("bvwo_done")
        s_ready = sem("constants_ready")
        x_loaded = [sem(f"x_loaded{p}") for p in range(2)]
        stored = [sem(f"stored{p}") for p in range(2)]
        done = {u: sem(f"{u}_done") for u in NAMES}
        drained = {u: sem(f"{u}_drained") for u in NAMES}
        upper_made = {u: sem(f"{u}_upper") for u in SPLIT}
        s_wcopied = sem("weight_upper")
        s_wsplit = sem("weight_split")
        N_WEIGHTS = 7
        s_whole = [sem(f"weight_loaded{n}") for n in range(N_WEIGHTS)]
        x0_upper = sem("x0_upper_made")
        x0_split = sem("x0_split")
        r0_made = sem("r0_made")
        t0_made = sem("t0_made")
        x1_made = sem("x1_made")
        x1b_made = sem("x1b_made")
        x2_made = sem("x2_made")
        x2b_made = sem("x2b_made")
        ox_made = sem("ox_made")
        w_made = sem("w_made")
        h2_made = sem("h2_made")
        x3_made = sem("x3_made")
        x3b_made = sem("x3b_made")
        out_made = sem("out_made")
        xin_made = {"a": x2_made, "c": x3_made}
        s_done = {L: sem(f"scores_{L}_done") for L in "ac"}
        masked, exped, inverted, normed, pT_done, pT_copied = ({} for _ in range(6))
        for L in "ac":
            masked[L] = sem(f"masked_{L}")
            exped[L] = sem(f"exped_{L}")
            inverted[L] = sem(f"inverted_{L}")
            normed[L] = sem(f"normed_{L}")
            pT_done[L] = [sem(f"pT_{L}_done{b}") for b in range(PAIR)]
            pT_copied[L] = [sem(f"pT_{L}_copied{b}") for b in range(PAIR)]
        stats_made = {n: sem(f"stats_{n}") for n in NORMS}
        aggr_made = {n: sem(f"aggr_{n}") for n in NORMS}
        var_made = {n: sem(f"var_{n}") for n in NORMS}
        rstd_made = {n: sem(f"rstd_{n}") for n in NORMS}

        def runs(stage, rep):
            return 0 <= rep - LAG[stage] < GROUPS

        def engine_program(eng, body):
            for i in range(PERIOD * HEAD_TURNS):
                body(i, i)
            with eng.Fori(HEAD_TURNS, GROUPS // PERIOD) as turn:
                for p in range(PERIOD):
                    body(turn * PERIOD + p, PERIOD * HEAD_TURNS + p)
            for i in range(GROUPS, GROUPS + LAST_LAG):
                body(i, i)

        def unit_head(u, n):
            return n // 2 * 4 + 2 * u + n % 2

        def bank(use):
            return GB[USES[NAMES.index(use)][2]]

        def wait_bank(pe, use, i, rep):
            n = rep * len(USES) + NAMES.index(use)
            for m in range(n - 1, -1, -1):
                before, stage, k = USES[m % len(USES)]
                then = m // len(USES)
                if k == USES[NAMES.index(use)][2] and runs(stage, then):
                    pe.wait_ge(drained[before], i - (rep - then) - LAG[stage] + 1)
                    return

        block = ctx.enter_context(nc.Block())

        def columns(pair, n):
            return tuple(w[:, :, n * D:(n + 1) * D] for w in pair)

        def staged(tile, at, n):
            flat = tile[:, :, :, :].rearrange("p b h n -> p (b h n)")
            return flat[:, at:at + DC * n].rearrange("p (c n) -> p c n", c=DC)

        W = DC * D
        wo3_sb = staged(E["c"], W, D)
        BY_UNIT = (wo3, wp2)
        SPLIT_WEIGHTS = [
            (w1, staged(nt["c"], 0, D), w1_sb),
            (wqkv2, staged(nt["a"], 0, 3 * D), wqkv_sb["a"]),
            (wp2, staged(nt["c"], W, D), wo_sb["a"]),
            (wq3, staged(nt["c"], 2 * W, D), columns(wqkv_sb["c"], 0)),
            (wk3, staged(nt["c"], 3 * W, D), columns(wqkv_sb["c"], 1)),
            (wv3, staged(E["c"], 0, D), columns(wqkv_sb["c"], 2)),
            (wo3, wo3_sb, wo_sb["c"]),
        ]
        assert len(SPLIT_WEIGHTS) == N_WEIGHTS
        ROWS = [(b1, b1_row), (bp2, bp2_row), (gam2, gam_row), (bet2, bet_row), (bo3, bo_row)]
        N_SMALL_DMAS = 2 * DC + 2 * DC + len(ROWS)

        def whole_loaded(n):
            return 16 * DC if SPLIT_WEIGHTS[n][0] in BY_UNIT else 16

        @block.sync
        def _(sp):
            sp.dma_start(adj_sb[:, :], adj).then_inc(s_adj, 16)
            sp.dma_start(b0_col[:, :], b0.rearrange("(p o) -> p o", o=1)).then_inc(s_b0, 16)

            def load_weight(n):
                src, whole, _ = SPLIT_WEIGHTS[n]
                if src in BY_UNIT:
                    for c in range(DC):
                        sp.dma_start(whole[c * P // 2:(c + 1) * P // 2, :, :],
                                     src[c * P:(c + 1) * P, :].rearrange("(u p) n -> p u n", p=P // 2)
                                     ).then_inc(s_whole[n], 16)
                else:
                    sp.dma_start(whole, src.rearrange("(c p) n -> p c n", p=P)).then_inc(s_whole[n], 16)

            def load_small():
                for src, dst in ROWS:
                    sp.dma_start(dst[:, :],
                                 src.rearrange("(o n) -> o n", o=1).to_broadcast([P, D])).then_inc(s_small, 16)
                for c in range(DC):
                    for u in range(2):
                        sp.dma_start(bv_col[c * P // 2:(c + 1) * P // 2, u:u + 1],
                                     bv3[(2 * c + u) * P // 2:(2 * c + u + 1) * P // 2]
                                     .rearrange("(p o) -> p o", o=1)).then_inc(s_small, 16)
                for dst, src in ((bq_col, bq3), (bk_col, bk3)):
                    for c in range(DC):
                        sp.dma_start(dst[:, c:c + 1],
                                     src[c * P:(c + 1) * P].rearrange("(p o) -> p o", o=1)).then_inc(s_small, 16)

            def body(i, rep):
                p = rep % 2
                if runs("L0", rep):
                    g = i
                    if rep >= 2:
                        sp.wait_ge(t0_made, 2 * (g - 1))
                        sp.wait_ge(x0_split, g - 1)
                    sp.dma_start(x0[:, p, :, :], x_v[g]).then_inc(x_loaded[p], 16)
                if rep == 0:
                    load_weight(0)
                if rep == 1:
                    load_weight(1)
                    load_small()
                    for n in range(2, N_WEIGHTS):
                        load_weight(n)
                if 0 <= rep - LAST_LAG < GROUPS:
                    g = i - LAST_LAG
                    sp.wait_ge(out_made, 2 * (g + 1))
                    q = (rep - LAST_LAG) % 2
                    sp.dma_start(out_v[g], out_sb[:, q, :, :]).then_inc(stored[q], 16)

            engine_program(sp, body)
            for p in range(2):
                sp.wait_ge(stored[p], 16 * GROUPS // 2)

        @block.tensor
        def _(pe):
            pe.wait_ge(s_ident, 2)
            pe.wait_ge(s_adj, 16)
            pe.transpose(PT[1][:, 0, :], adj_sb[:, :], ident[:, :]).then_inc(s_adjT, 1)
            pe.wait_ge(s_adjTc, 3)

            def bias_through_projection():
                pe.wait_ge(s_setup, DC)
                pe.wait_ge(s_whole[N_WEIGHTS - 1], whole_loaded(N_WEIGHTS - 1))
                for c in range(DC):
                    last = pe.matmul(PT[0][:, 0:2, :], bv_wide[:, c, :], wo3_sb[:, c, :],
                                     start=(c == 0), stop=(c == DC - 1))
                last.then_inc(s_bvwo, 1)

            def transpose_input(L, i, rep):
                if not runs(L, rep):
                    return
                g, p = i - LAG[L], (rep - LAG[L]) % 2
                o = bank(f"xT_{L}")
                wait_bank(pe, f"xT_{L}", i, rep)
                pe.wait_ge(xin_made[L], 2 * (g + 1))
                for c in range(DC):
                    for b in range(PAIR):
                        n = c * PAIR + b
                        last = pe.transpose(o[:, n * N:(n + 1) * N], xin[L][:, p, b, c * P:(c + 1) * P],
                                            ident[:, :])
                last.then_inc(done[f"xT_{L}"], 1)

            def queries(L, i, rep):
                project_T("q", 0, L, i, rep)

            def keys(L, i, rep):
                project_T("k", 1, L, i, rep)

            def project_T(what, n, L, i, rep):
                if not runs(L, rep):
                    return
                w = columns(wqkv_sb[L], n)
                o = bank(f"{what}_{L}")
                wait_bank(pe, f"{what}_{L}", i, rep)
                g = i - LAG[L]
                pe.wait_ge(upper_made[f"xT_{L}"], g + 1)
                for m in range(DC):
                    for part, (s, x) in enumerate(((0, 0), (1, 0), (0, 1))):
                        if m == 0 and part == 2:
                            pe.wait_ge(drained[f"xT_{L}"], g + 1)
                        for c in range(DC):
                            last = pe.matmul(o[:, m * PAIR * N:(m + 1) * PAIR * N],
                                             w[s][:, c, m * P:(m + 1) * P], xT[L][x][:, c, :],
                                             start=(part == 0 and c == 0), stop=(part == 2 and c == DC - 1))
                last.then_inc(done[f"{what}_{L}"], 1)

            def rows_product(o, data, w, lower, value):
                for b in range(PAIR):
                    for part, (x, s) in enumerate(((0, 0), (0, 1), (1, 0))):
                        if b == 0 and part == 2:
                            pe.wait_ge(lower, value)
                        for c in range(DC):
                            last = pe.matmul(o[:, b * D:(b + 1) * D], data(x, b, c), w[s][:, c, :],
                                             start=(part == 0 and c == 0), stop=(part == 2 and c == DC - 1))
                return last

            def project_v(L, i, rep):
                if not runs(L, rep):
                    return
                wait_bank(pe, f"v_{L}", i, rep)
                rows_product(bank(f"v_{L}"), lambda x, b, c: xT[L][x][:, c, b * N:(b + 1) * N],
                             columns(wqkv_sb[L], 2), drained[f"xT_{L}"],
                             i - LAG[L] + 1).then_inc(done[f"v_{L}"], 1)

            def scores(L, u, stage, i, rep):
                if not runs(stage, rep):
                    return
                g = i - LAG[stage]
                if u == 0:
                    pe.wait_ge(drained[f"q_{L}"], g + 1)
                    pe.wait_ge(drained[f"k_{L}"], g + 1)
                M, other, back = ("a", "a_tail", 0) if L == "c" else ("c", "c", u)
                if runs(other, rep - back):
                    pe.wait_ge(masked[M], 2 * (i - back - LAG[other]) + u + 1)
                elif rep - LAG[stage] >= 1:
                    pe.wait_ge(masked[L], 2 * (g - 1) + u + 1)
                for b in range(PAIR):
                    for c in range(DC):
                        for r in (2 * u, 2 * u + 1):
                            rows = slice(32 * r, 32 * r + 32)
                            n = (b * DC + c) * N
                            last = pe.matmul(S[:, r, n:n + N], qT[L][rows, c, b * N:(b + 1) * N],
                                             kT[L][rows, c, b * N:(b + 1) * N], start=True, stop=True)
                last.then_inc(s_done[L], 1)

            def turn(L, u, b, i, rep):
                stage = f"{L}_tail"
                if not runs(stage, rep):
                    return
                g = i - LAG[stage]
                pe.wait_ge(normed[L], 2 * g + u + 1)
                M, back = ("c", 0) if L == "a" else ("a", 1)
                if u == 1:
                    pe.wait_ge(pT_copied[L][b], 2 * g + 1)
                elif runs(f"{M}_tail", rep - back):
                    pe.wait_ge(pT_copied[M][b], 2 * (i - back - LAG[f"{M}_tail"] + 1))
                elif rep - LAG[stage] >= 1:
                    pe.wait_ge(pT_copied[L][b], 2 * g)
                for n in range(4):
                    last = pe.transpose(PT[b][:, n, :], E[L][:, u, 4 * b + n, :], ident[:, :])
                last.then_inc(pT_done[L][b], 1)

            def values(L, u, b, i, rep):
                stage = f"{L}_tail"
                if not runs(stage, rep):
                    return
                g = i - LAG[stage]
                if (u, b) == (0, 0):
                    wait_bank(pe, f"pv_{L}", i, rep)
                    pe.wait_ge(drained[f"v_{L}"], g + 1)
                pe.wait_ge(pT_copied[L][b], 2 * g + u + 1)
                o = bank(f"pv_{L}")
                at = (b * DC + u) * N
                for n in range(4):
                    h = unit_head(u, n)
                    last = pe.matmul(o[32 * n:32 * n + 32, at:at + N], v[L][:, b, h * HD:(h + 1) * HD],
                                     pT[u][b][:, n, :], start=True, stop=True)
                if (u, b) == (1, PAIR - 1):
                    last.then_inc(done[f"pv_{L}"], 1)

            def project_out(L, i, rep):
                stage = f"{L}_tail"
                if not runs(stage, rep):
                    return
                g = i - LAG[stage]
                wait_bank(pe, f"proj_{L}", i, rep)
                pe.wait_ge(upper_made[f"pv_{L}"], g + 1)
                rows_product(bank(f"proj_{L}"), lambda x, b, c: oT[x][:, b, c, :], wo_sb[L],
                             drained[f"pv_{L}"], g + 1).then_inc(done[f"proj_{L}"], 1)

            def l1_neighbours(i, rep):
                if not runs("L1", rep):
                    return
                g, p = i - LAG["L1"], (rep - LAG["L1"]) % 2
                o = bank("yT")
                wait_bank(pe, "yT", i, rep)
                pe.wait_ge(x1_made, 2 * (g + 1))
                for b in range(PAIR):
                    for c in range(DC):
                        n = b * DC + c
                        last = pe.matmul(o[:, n * N:(n + 1) * N], x1[:, p, b, c * P:(c + 1) * P], adjT[:, :],
                                         start=True, stop=True)
                last.then_inc(done["yT"], 1)

            def l1_weight(i, rep):
                if not runs("L1", rep):
                    return
                g = i - LAG["L1"]
                wait_bank(pe, "h1", i, rep)
                pe.wait_ge(upper_made["yT"], g + 1)
                rows_product(bank("h1"), lambda x, b, c: yT[x][:, b, c, :], w1_sb,
                             drained["yT"], g + 1).then_inc(done["h1"], 1)

            def l0_product(i, rep):
                if not runs("L0", rep):
                    return
                wait_bank(pe, "A0", i, rep)
                pe.wait_ge(x0_split, i + 1)
                for part, (a, x) in enumerate(((0, 0), (0, 1), (1, 0))):
                    last = pe.matmul(bank("A0")[:, :], adjT_h[a][:, :], x0_h[x][:, :, :],
                                     start=(part == 0), stop=(part == 2))
                last.then_inc(done["A0"], 1)

            def body(i, rep):
                if rep == LAG["L1"]:
                    pe.wait_ge(s_wsplit, 1)
                if rep == LAG["a"]:
                    pe.wait_ge(s_wsplit, 2)
                    bias_through_projection()
                if rep == LAG["a_tail"]:
                    pe.wait_ge(s_ready, 1)
                for L, filler in (("c", l1_neighbours), ("a", l0_product)):
                    turn(L, 0, 0, i, rep)
                    turn(L, 0, 1, i, rep)
                    filler(i, rep)
                    values(L, 0, 0, i, rep)
                    turn(L, 1, 0, i, rep)
                    turn(L, 1, 1, i, rep)
                    values(L, 0, 1, i, rep)
                    transpose_input(L, i, rep)
                    values(L, 1, 0, i, rep)
                    values(L, 1, 1, i, rep)
                    M, stage = ("a", "a_tail") if L == "c" else ("c", "c")
                    scores(M, 1, stage, i, rep)
                    queries(L, i, rep)
                    keys(L, i, rep)
                    project_out(L, i, rep)
                    project_v(L, i, rep)
                    if L == "c":
                        l1_weight(i, rep)
                    scores(L, 0, L, i, rep)

            engine_program(pe, body)

        @block.scalar
        def _(act):
            def split_weights(first, end):
                for n in range(first, end):
                    _, whole, dst = SPLIT_WEIGHTS[n]
                    act.wait_ge(s_whole[n], whole_loaded(n))
                    act.copy(dst[0][:, :, :], whole).then_inc(s_wcopied, 1)

            split_weights(0, 1)

            def upper_half(use, stage, i, rep):
                if not runs(stage, rep):
                    return
                g = i - LAG[stage]
                act.wait_ge(done[use], g + 1)
                dst = SPLIT[use][0]
                act.copy(dst[:, :, :] if len(dst.shape) == 3 else dst[:, :, :, :],
                         bank(use)[:, :]).then_inc(upper_made[use], 1)

            def drain_q(L, i, rep):
                if not runs(L, rep):
                    return
                g = i - LAG[L]
                o = bank(f"q_{L}")
                act.wait_ge(done[f"q_{L}"], g + 1)
                if L == "a":
                    act.mul(qT[L][:, :, :], o[:, :], SCALE).then_inc(drained["q_a"], 1)
                else:
                    for c in range(DC):
                        last = act.activation(qT[L][:, c, :], o[:, c * PAIR * N:(c + 1) * PAIR * N],
                                              ACT.Identity, scale=SCALE, bias=bq_col[:, c:c + 1])
                    last.then_inc(drained["q_c"], 1)

            def drain_v(L, i, rep):
                if not runs(L, rep):
                    return
                g = i - LAG[L]
                act.wait_ge(done[f"v_{L}"], g + 1)
                act.copy(v[L][:, :, :], bank(f"v_{L}")[:, :]).then_inc(drained[f"v_{L}"], 1)

            def exps(L, u, part, stage, i, rep):
                if not runs(stage, rep):
                    return
                g = i - LAG[stage]
                if part == 0:
                    act.wait_ge(masked[L], 2 * g + u + 1)
                    if rep - LAG[stage] >= 1:
                        for b in range(PAIR):
                            act.wait_ge(pT_done[L][b], 2 * (g - 1) + u + 1)
                        act.wait_ge(inverted[L], 2 * (g - 1) + u + 1)
                for h in range(part * UNIT_HEADS // 2, (part + 1) * UNIT_HEADS // 2):
                    last = act.activation(E[L][:, u, h, :], nt[L][:, u, h, :], ACT.Exp, scale=-1.0,
                                          bias=nmax[L][:, u, h:h + 1], accum_out=esum[L][:, u, h:h + 1])
                if part == 1:
                    last.then_inc(exped[L], 1)

            def drain_pT(L, u, b, i, rep):
                stage = f"{L}_tail"
                if not runs(stage, rep):
                    return
                g = i - LAG[stage]
                act.wait_ge(pT_done[L][b], 2 * g + u + 1)
                act.copy(pT[u][b][:, :, :], PT[b][:, :, :]).then_inc(pT_copied[L][b], 1)

            def add_r0(i, rep):
                if not runs("L0", rep):
                    return
                p = rep % 2
                act.wait_ge(r0_made, i + 1)
                if rep >= 1:
                    act.wait_ge(x1_made, 2 * i)
                for b in range(PAIR):
                    act.activation(t0[:, b, :], x0[:, p, b, :], ACT.Identity,
                                   bias=r0[:, b:b + 1]).then_inc(t0_made, 1)

            def body(i, rep):
                if rep == LAG["a_tail"]:
                    act.wait_ge(s_ready, 1)
                for L in "ca":
                    drain_pT(L, 0, 0, i, rep)
                    drain_pT(L, 0, 1, i, rep)
                    if L == "c":
                        upper_half("yT", "L1", i, rep)
                    drain_pT(L, 1, 0, i, rep)
                    drain_pT(L, 1, 1, i, rep)
                    upper_half(f"xT_{L}", L, i, rep)
                    upper_half(f"pv_{L}", f"{L}_tail", i, rep)
                    if L == "a":
                        add_r0(i, rep)
                    M, stage = ("a", "a_tail") if L == "c" else ("c", "c")
                    exps(M, 0, 0, stage, i, rep)
                    drain_q(L, i, rep)
                    exps(M, 0, 1, stage, i, rep)
                    exps(M, 1, 0, stage, i, rep)
                    exps(M, 1, 1, stage, i, rep)
                    drain_v(L, i, rep)
                if rep == 0:
                    split_weights(1, 3)
                if rep == 1:
                    split_weights(3, N_WEIGHTS)

            engine_program(act, body)

        @block.vector
        def _(dve):
            dve.memset(neg_half[:, :], -0.5).then_inc(s_half, 1)
            dve.memset(ones[:, :], 1.0).then_inc(s_ones, 1)
            dve.wait_ge(s_adjT, 1)
            dve.tensor_copy(adjT[:, :], PT[1][:, 0, :]).then_inc(s_adjTc, 1)
            dve.wait_ge(s_adjTc, 1)
            dve.tensor_copy(adjT_h[0][:, :], adjT[:, :]).then_inc(s_adjTc, 1)
            dve.wait_ge(s_adjTc, 2)
            dve.tensor_tensor(adjT_h[1][:, :], adjT[:, :], adjT_h[0][:, :].bitcast(F32),
                              ALU.subtract).then_inc(s_adjTc, 1)
            dve.wait_ge(s_b0, 16)

            def split_weights(first, end):
                for n in range(first, end):
                    _, whole, dst = SPLIT_WEIGHTS[n]
                    dve.wait_ge(s_whole[n], whole_loaded(n))
                    dve.wait_ge(s_wcopied, n + 1)
                    dve.tensor_tensor(dst[1][:, :, :], whole,
                                      dst[0][:, :, :].bitcast(F32), ALU.subtract).then_inc(s_wsplit, 1)

            def first_constants():
                dve.wait_ge(s_ones, 1)
                dve.wait_ge(s_small, 16 * N_SMALL_DMAS)
                dve.wait_ge(s_adj, 16)
                for c in range(DC):
                    dve.tensor_scalar(bv_wide[:, c, :], ones[:, :], bv_col[:, c:c + 1], None,
                                      ALU.mult).then_inc(s_setup, 1)
                dve.tensor_scalar(bias["a"][:, :], adj_sb[:, :], 0.0, NEG_BIG, ALU.is_equal,
                                  ALU.mult).then_inc(s_setup, 1)
                dve.tensor_scalar(bias["c"][:, :], adj_sb[:, :], -1.0, 1.0, ALU.mult, ALU.add).then_inc(s_setup, 1)
                dve.tensor_scalar(bq_col[:, :], bq_col[:, :], SCALE, None, ALU.mult).then_inc(s_setup, 1)
                dve.wait_ge(s_setup, DC + 3)
                dve.tensor_scalar(bias["c"][:, :], bias["c"][:, :], -1e9, None, ALU.mult).then_inc(s_setup, 1)

            def last_constants():
                dve.wait_ge(s_bvwo, 1)
                dve.tensor_tensor(bo_row[:, :], PT[0][:, 0:2, :].rearrange("p a n -> p (a n)"), bo_row[:, :],
                                  ALU.add).then_inc(s_setup, 1)
                dve.wait_ge(s_setup, DC + 5)
                dve.wait_ge(s_wsplit, N_WEIGHTS)
                dve.memset(gate[:, :], 0.0).then_inc(s_ready, 1)
                dve.wait_ge(s_ready, 1)

            def statistics(norm, src, g):
                for b in range(PAIR):
                    dve.bn_stats(st[norm][:, b, :], src[:, b, :]).then_inc(stats_made[norm], 1)
                dve.wait_ge(stats_made[norm], 2 * (g + 1))
                dve.memset(gate[:, :], 0.0)
                for b in range(PAIR):
                    dve.bn_aggr(mv[norm][:, b, :], st[norm][:, b, :]).then_inc(aggr_made[norm], 1)
                dve.wait_ge(aggr_made[norm], 2 * (g + 1))
                dve.tensor_scalar(ve[norm][:, :], mv[norm][:, :, 1], LN_EPS, None,
                                  ALU.add).then_inc(var_made[norm], 1)

            def normalise(norm, dst, src, g, made):
                dve.wait_ge(rstd_made[norm], g + 1)
                for b in range(PAIR):
                    dve.tensor_scalar(dst[:, b, :], src[:, b, :], mv[norm][:, b, 0:1], rstd[norm][:, b:b + 1],
                                      ALU.subtract, ALU.mult).then_inc(made, 1)

            def lower_half(use, stage, i, rep):
                if not runs(stage, rep):
                    return
                g = i - LAG[stage]
                dve.wait_ge(upper_made[use], g + 1)
                upper, lower = SPLIT[use]
                every = (slice(None),) * len(upper.shape)
                dve.tensor_tensor(lower[every], bank(use)[:, :], upper[every].bitcast(F32),
                                  ALU.subtract).then_inc(drained[use], 1)

            def drain_k(L, i, rep):
                if not runs(L, rep):
                    return
                g = i - LAG[L]
                o = bank(f"k_{L}")
                dve.wait_ge(done[f"k_{L}"], g + 1)
                if L == "a":
                    dve.tensor_copy(kT[L][:, :, :], o[:, :]).then_inc(drained["k_a"], 1)
                else:
                    for c in range(DC):
                        last = dve.tensor_scalar(kT[L][:, c, :], o[:, c * PAIR * N:(c + 1) * PAIR * N],
                                                 bk_col[:, c:c + 1], None, ALU.add)
                    last.then_inc(drained["k_c"], 1)

            def mask(L, u, stage, i, rep):
                if not runs(stage, rep):
                    return
                g = i - LAG[stage]
                dve.wait_ge(s_done[L], 2 * g + u + 1)
                if rep - LAG[stage] >= 1:
                    dve.wait_ge(exped[L], 2 * (g - 1) + u + 1)
                column = "ac".index(L) * 2 + u
                dve.memset(gate_m[:, column:column + 1], 0.0)
                for n in range(UNIT_HEADS):
                    b, c, r = n // 4, n // 2 % 2, 2 * u + n % 2
                    at = (b * DC + c) * N
                    last = dve.tensor_tensor_reduce(nt[L][:, u, n, :], S[:, r, at:at + N], bias[L][:, :],
                                                    -1.0, FAR, ALU.add, ALU.min, nmax[L][:, u, n:n + 1])
                last.then_inc(masked[L], 1)

            def invert(L, u, stage, i, rep):
                if not runs(stage, rep):
                    return
                g = i - LAG[stage]
                dve.wait_ge(exped[L], 2 * g + u + 1)
                if rep - LAG[stage] >= 1:
                    dve.wait_ge(normed[L], 2 * (g - 1) + u + 1)
                dve.reciprocal(rinv[L][:, u, :], esum[L][:, u, :]).then_inc(inverted[L], 1)

            def l3_residual(i, rep):
                if not runs("c_tail", rep):
                    return
                g, p = i - LAG["c_tail"], (rep - LAG["c_tail"]) % 2
                dve.wait_ge(done["proj_c"], g + 1)
                dve.wait_ge(x3b_made, g + 1)
                if rep - LAG["c_tail"] >= 1:
                    dve.wait_ge(out_made, 2 * g)
                dve.tensor_tensor(h3[:, :, :], bank("proj_c")[:, :], x3b[:, p, :, :],
                                  ALU.add).then_inc(drained["proj_c"], 1)

            def l3_statistics(i, rep):
                if not runs("c_tail", rep):
                    return
                g = i - LAG["c_tail"]
                dve.wait_ge(drained["proj_c"], g + 1)
                statistics("nc", h3, g)

            def l3_out(i, rep):
                if not runs("c_tail", rep):
                    return
                g, p = i - LAG["c_tail"], (rep - LAG["c_tail"]) % 2
                if rep - LAG["c_tail"] >= 2:
                    dve.wait_ge(stored[p], (g - p) * 8)
                normalise("nc", out_sb[:, p, :, :], h3, g, out_made)

            def l1_residual(i, rep):
                if not runs("L1", rep):
                    return
                g = i - LAG["L1"]
                dve.wait_ge(done["h1"], g + 1)
                dve.wait_ge(x1b_made, g + 1)
                if rep - LAG["L1"] >= 1:
                    dve.wait_ge(x2_made, 2 * g)
                dve.tensor_tensor(h1[:, :, :], bank("h1")[:, :], x1b[:, :, :],
                                  ALU.add).then_inc(drained["h1"], 1)

            def l1_statistics(i, rep):
                if not runs("L1", rep):
                    return
                g = i - LAG["L1"]
                dve.wait_ge(drained["h1"], g + 1)
                statistics("n1", h1, g)

            def l1_out(i, rep):
                if not runs("L1", rep):
                    return
                g, p = i - LAG["L1"], (rep - LAG["L1"]) % 2
                if rep - LAG["L1"] >= 2:
                    dve.wait_ge(done["xT_a"], g - 1)
                    dve.wait_ge(x2b_made, g - 1)
                normalise("n1", x2[:, p, :, :], h1, g, x2_made)

            def l0_max(i, rep):
                if not runs("L0", rep):
                    return
                dve.wait_ge(done["A0"], i + 1)
                if rep >= 1:
                    dve.wait_ge(r0_made, i)
                dve.tensor_reduce(mx0[:, :], bank("A0")[:, :].rearrange("p (b n) -> p b n", b=PAIR),
                                  AX_X, ALU.max).then_inc(drained["A0"], 1)
                dve.wait_ge(drained["A0"], i + 1)
                if rep >= 1:
                    dve.wait_ge(t0_made, 2 * i)
                dve.tensor_scalar(r0[:, :], mx0[:, :], b0_col[:, 0:1], 0.0, ALU.add,
                                  ALU.max).then_inc(r0_made, 1)

            def l0_statistics(i, rep):
                if not runs("L0", rep):
                    return
                dve.wait_ge(t0_made, 2 * (i + 1))
                statistics("n0", t0, i)

            def l0_out(i, rep):
                if not runs("L0", rep):
                    return
                p = rep % 2
                if rep >= 2:
                    dve.wait_ge(done["yT"], i - 1)
                    dve.wait_ge(x1b_made, i - 1)
                normalise("n0", x1[:, p, :, :], t0, i, x1_made)

            def l2_bias(i, rep):
                if not runs("a_tail", rep):
                    return
                g = i - LAG["a_tail"]
                dve.wait_ge(done["proj_a"], g + 1)
                if rep - LAG["a_tail"] >= 1:
                    dve.wait_ge(w_made, 2 * g)
                    dve.wait_ge(ox_made, g)
                dve.tensor_tensor(o_sb[:, :, :],
                                  bank("proj_a")[:, :].rearrange("p (b n) -> p b n", b=PAIR),
                                  bp2_row[:, :].unsqueeze(1).to_broadcast([P, PAIR, D]),
                                  ALU.add).then_inc(drained["proj_a"], 1)

            def inner_statistics(i, rep):
                if not runs("a_tail", rep):
                    return
                g = i - LAG["a_tail"]
                dve.wait_ge(drained["proj_a"], g + 1)
                statistics("ni", o_sb, g)

            def l2_scale(i, rep):
                if not runs("a_tail", rep):
                    return
                g = i - LAG["a_tail"]
                dve.wait_ge(aggr_made["ni"], 2 * (g + 1))
                if rep - LAG["a_tail"] >= 1:
                    dve.wait_ge(h2_made, 2 * g)
                for b in range(PAIR):
                    dve.scalar_tensor_tensor(out=w_ln[:, b, :], in0=o_sb[:, b, :], scalar=mv["ni"][:, b, 0:1],
                                             in1=gam_row[:, :], op0=ALU.subtract,
                                             op1=ALU.mult).then_inc(w_made, 1)

            def l2_sum(i, rep):
                if not runs("a_out", rep):
                    return
                g = i - LAG["a_out"]
                dve.wait_ge(w_made, 2 * (g + 1))
                dve.wait_ge(rstd_made["ni"], g + 1)
                dve.wait_ge(ox_made, g + 1)
                if rep - LAG["a_out"] >= 1:
                    dve.wait_ge(x3_made, 2 * g)
                for b in range(PAIR):
                    dve.scalar_tensor_tensor(out=h2[:, b, :], in0=w_ln[:, b, :], scalar=rstd["ni"][:, b:b + 1],
                                             in1=ox[:, b, :], op0=ALU.mult, op1=ALU.add).then_inc(h2_made, 1)

            def outer_statistics(i, rep):
                if not runs("a_out", rep):
                    return
                g = i - LAG["a_out"]
                dve.wait_ge(h2_made, 2 * (g + 1))
                statistics("no", h2, g)

            def l2_out(i, rep):
                if not runs("a_out", rep):
                    return
                g, p = i - LAG["a_out"], (rep - LAG["a_out"]) % 2
                if rep - LAG["a_out"] >= 2:
                    dve.wait_ge(done["xT_c"], g - 1)
                    dve.wait_ge(x3b_made, g - 1)
                normalise("no", x3[:, p, :, :], h2, g, x3_made)

            def body(i, rep):
                lower_half("yT", "L1", i, rep)
                mask("a", 0, "a_tail", i, rep)
                lower_half("xT_c", "c", i, rep)
                lower_half("pv_c", "c_tail", i, rep)
                mask("a", 1, "a_tail", i, rep)
                l2_sum(i, rep)
                drain_k("c", i, rep)
                invert("a", 0, "a_tail", i, rep)
                l3_residual(i, rep)
                outer_statistics(i, rep)
                l1_residual(i, rep)
                invert("a", 1, "a_tail", i, rep)
                l1_statistics(i, rep)
                l3_statistics(i, rep)
                l0_max(i, rep)
                l1_out(i, rep)
                mask("c", 0, "c", i, rep)
                lower_half("xT_a", "a", i, rep)
                lower_half("pv_a", "a_tail", i, rep)
                l0_statistics(i, rep)
                mask("c", 1, "c", i, rep)
                drain_k("a", i, rep)
                l2_out(i, rep)
                invert("c", 0, "c", i, rep)
                l0_out(i, rep)
                l2_bias(i, rep)
                l3_out(i, rep)
                invert("c", 1, "c", i, rep)
                inner_statistics(i, rep)
                l2_scale(i, rep)
                if rep == 0:
                    split_weights(0, 2)
                if rep == 1:
                    first_constants()
                    split_weights(2, N_WEIGHTS)
                if rep == 2:
                    last_constants()

            engine_program(dve, body)

        @block.gpsimd
        def _(pool):
            pool.memset(ident[:, :], 0.0).then_inc(s_ident, 1)
            pool.wait_ge(s_ident, 1)
            pool.affine_select(out=ident[:, :], in_=ident[:, :], compare_op=ALU.not_equal, fill=1.0,
                               base=0, pattern=[[-1, P]], channel_multiplier=1).then_inc(s_ident, 1)
            pool.wait_ge(s_half, 1)
            pool.wait_ge(s_ones, 1)

            def normalise(L, u, stage, i, rep):
                if not runs(stage, rep):
                    return
                pool.wait_ge(inverted[L], 2 * (i - LAG[stage]) + u + 1)
                pool.tensor_tensor(E[L][:, u, :, :], E[L][:, u, :, :],
                                   rinv[L][:, u, :].unsqueeze(2).to_broadcast([P, UNIT_HEADS, N]),
                                   ALU.mult).then_inc(normed[L], 1)

            def add_row(dst, src, row):
                return pool.tensor_tensor(dst, src, row[:, :].unsqueeze(1).to_broadcast([P, PAIR, D]), ALU.add)

            def power(norm, stage, i, rep):
                if not runs(stage, rep):
                    return
                g = i - LAG[stage]
                pool.wait_ge(var_made[norm], g + 1)
                pool.tensor_tensor(rstd[norm][:, :], ve[norm][:, :], neg_half[:, :],
                                   ALU.pow).then_inc(rstd_made[norm], 1)

            def split_x0(i, rep):
                if not runs("L0", rep):
                    return
                p = rep % 2
                pool.wait_ge(x_loaded[p], (i - p) * 8 + 16)
                if rep >= 1:
                    pool.wait_ge(done["A0"], i)
                pool.tensor_tensor(x0_h[0][:, :, :].rearrange("p b (c n) -> p (b c) n", c=DC),
                                   x0[:, p, :, :].rearrange("p b (c n) -> p (b c) n", c=DC),
                                   ones[:, :].unsqueeze(1).to_broadcast([P, PAIR * DC, P]),
                                   ALU.mult).then_inc(x0_upper, 1)
                pool.wait_ge(x0_upper, i + 1)
                pool.tensor_tensor(x0_h[1][:, :, :], x0[:, p, :, :], x0_h[0][:, :, :].bitcast(F32),
                                   ALU.subtract).then_inc(x0_split, 1)

            def add_b1(i, rep):
                if not runs("L1", rep):
                    return
                g, p = i - LAG["L1"], (rep - LAG["L1"]) % 2
                pool.wait_ge(x1_made, 2 * (g + 1))
                if rep - LAG["L1"] >= 1:
                    pool.wait_ge(drained["h1"], g)
                add_row(x1b[:, :, :], x1[:, p, :, :], b1_row).then_inc(x1b_made, 1)

            def add_beta(i, rep):
                if not runs("a", rep):
                    return
                g, p = i - LAG["a"], (rep - LAG["a"]) % 2
                pool.wait_ge(x2_made, 2 * (g + 1))
                if rep - LAG["a"] >= 2:
                    pool.wait_ge(ox_made, g - 1)
                add_row(x2b[:, p, :, :], x2[:, p, :, :], bet_row).then_inc(x2b_made, 1)

            def add_bo(i, rep):
                if not runs("c", rep):
                    return
                g, p = i - LAG["c"], (rep - LAG["c"]) % 2
                pool.wait_ge(x3_made, 2 * (g + 1))
                if rep - LAG["c"] >= 2:
                    pool.wait_ge(drained["proj_c"], g - 1)
                add_row(x3b[:, p, :, :], x3[:, p, :, :], bo_row).then_inc(x3b_made, 1)

            def add_o(i, rep):
                if not runs("a_out", rep):
                    return
                g, p = i - LAG["a_out"], (rep - LAG["a_out"]) % 2
                pool.wait_ge(drained["proj_a"], g + 1)
                pool.wait_ge(x2b_made, g + 1)
                if rep - LAG["a_out"] >= 1:
                    pool.wait_ge(h2_made, 2 * g)
                pool.tensor_tensor(ox[:, :, :], o_sb[:, :, :], x2b[:, p, :, :], ALU.add).then_inc(ox_made, 1)

            def body(i, rep):
                if rep == LAG["L1"]:
                    pool.wait_ge(s_small, 16 * N_SMALL_DMAS)
                if rep == LAG["a_tail"]:
                    pool.wait_ge(s_ready, 1)
                power("ni", "a_out", i, rep)
                add_o(i, rep)
                add_b1(i, rep)
                add_bo(i, rep)
                split_x0(i, rep)
                normalise("a", 0, "a_tail", i, rep)
                power("no", "a_out", i, rep)
                normalise("a", 1, "a_tail", i, rep)
                power("n1", "L1", i, rep)
                power("nc", "c_tail", i, rep)
                add_beta(i, rep)
                power("n0", "L0", i, rep)
                normalise("c", 0, "c", i, rep)
                normalise("c", 1, "c", i, rep)

            engine_program(pool, body)


_INS = ['x', 'adj', 'L0_gnn_b', 'L1_gnn_weight', 'L1_gnn_bias', 'L2_gnn_w_qkv', 'L2_gnn_w_proj',
        'L2_gnn_b_proj', 'L2_gnn_ln_gamma', 'L2_gnn_ln_beta', 'L3_gnn_Wq', 'L3_gnn_bq', 'L3_gnn_Wk',
        'L3_gnn_bk', 'L3_gnn_Wv', 'L3_gnn_bv', 'L3_gnn_Wo', 'L3_gnn_bo']


def kernel(**inputs):
    import numpy as _np
    import concourse.bacc as _bacc
    from concourse import mybir as _mybir
    from concourse.bass_utils import run_bass_kernel_spmd as _run

    nc = _bacc.Bacc("TRN2", target_bir_lowering=False, num_devices=1)
    arrays, args = {}, []
    for name in _INS:
        a = _np.ascontiguousarray(inputs[name])
        arrays[f"in_{name}_dram"] = a
        args.append(nc.dram_tensor(f"in_{name}_dram", a.shape, _mybir.dt.from_np(a.dtype), kind="ExternalInput").ap())
    shape = inputs['x'].shape
    args.append(nc.dram_tensor("out_0_dram", shape, _mybir.dt.float32, kind="ExternalOutput").ap())
    gnn_stack_kernel(nc, *args)
    r = _run(nc, [arrays], core_ids=[0])
    return r.results[0]["out_0_dram"]
```
